# Optimizing a Trainium2 kernel written in Bass

```python
import numpy as np
import jax
import jax.numpy as jnp

def _softmax(x, axis=-1):
    return jax.nn.softmax(x, axis=axis)

def _gelu(x):
    return jax.nn.gelu(x, approximate=True)

def _silu(x):
    return jax.nn.silu(x)

def _sigmoid(x):
    return jax.nn.sigmoid(x)

def _layernorm(x, axis=-1, eps=1e-05):
    m = jnp.mean(x, axis=axis, keepdims=True)
    v = jnp.var(x, axis=axis, keepdims=True)
    return (x - m) / jnp.sqrt(v + eps)

def _scatter_add(tgt, idx, src, axis=0):
    return tgt.at[idx].add(src)

def _segment_sum(src, seg, n):
    return jax.ops.segment_sum(src, seg, n)
kernel_name = 'mk_macaron_d1_jaxref_r4_9d2037'

def setup_inputs(seed: int=0):
    np.random.seed(seed)
    _w = jnp.asarray

    def _L0_attn_setup():
        import jax, jax.numpy as jnp
        import numpy as np
        B_, L_, D_, E_, N_, DR_, DC_ = (2, 512, 256, 512, 16, 64, 4)
        key = jax.random.key(seed)
        ks = jax.random.split(key, 12)
        s = lambda fan: 1.0 / np.sqrt(fan)
        inp = {}
        inp['resid'] = jax.random.normal(ks[0], (B_, L_, D_), jnp.float32)
        inp['norm_w'] = jnp.ones((D_,), jnp.float32)
        inp['skip_w'] = jax.random.normal(ks[1], (E_, D_), jnp.float32) * s(D_)
        inp['in_w'] = jax.random.normal(ks[2], (E_, D_), jnp.float32) * s(D_)
        inp['conv_w'] = jax.random.normal(ks[3], (E_, DC_), jnp.float32) * s(DC_)
        inp['conv_b'] = jax.random.normal(ks[4], (E_,), jnp.float32) * 0.1
        inp['wd1'] = jax.random.normal(ks[5], (DR_, E_), jnp.float32) * s(E_)
        inp['wd2'] = jax.random.uniform(ks[6], (E_, DR_), jnp.float32, -1.0, 1.0) * DR_ ** (-0.5)
        dt = jnp.exp(jax.random.uniform(ks[7], (E_,), jnp.float32) * (np.log(0.1) - np.log(0.001)) + np.log(0.001))
        dt = jnp.clip(dt, 0.0001, None)
        inp['wd2_b'] = dt + jnp.log(-jnp.expm1(-dt))
        inp['wB'] = jax.random.normal(ks[8], (N_, E_), jnp.float32) * s(E_)
        inp['wC'] = jax.random.normal(ks[9], (N_, E_), jnp.float32) * s(E_)
        inp['A_log'] = jnp.log(jnp.broadcast_to(jnp.arange(1, N_ + 1, dtype=jnp.float32), (E_, N_)))
        inp['W_D'] = jnp.ones((E_,), jnp.float32)
        inp['out_w'] = jax.random.normal(ks[10], (D_, E_), jnp.float32) * s(E_)
        return inp
    _L0_attn_in = _L0_attn_setup()

    def _L0_ffn_setup():
        import jax, jax.numpy as jnp
        import numpy as np
        B, S, DIM = (4, 1024, 256)
        BASE_COUPLING = 0.1
        NUM_CYCLES = 3

        def _gelu(x):
            return jax.nn.gelu(x, approximate=False)

        def _coupling_net(h, w1, b1, w2, b2, w3, b3, w4, b4):
            h = _gelu(h @ w1 + b1)
            h = _gelu(h @ w2 + b2)
            h = _gelu(h @ w3 + b3)
            return jax.nn.sigmoid(h @ w4 + b4)

        def _global_net(h, w1, b1, w2, b2, w3, b3):
            h = _gelu(h @ w1 + b1)
            h = _gelu(h @ w2 + b2)
            return jax.nn.sigmoid(h @ w3 + b3)

        def _twist(x):
            o_r, o_i, p_r, p_i = jnp.split(x, 4, axis=-1)
            return jnp.concatenate([p_r, -p_i, -o_r, o_i], axis=-1)
        key = jax.random.key(seed)
        ks = jax.random.split(key, 9)
        d = DIM

        def w(k, fan_in, fan_out):
            return jax.random.normal(k, (fan_in, fan_out), dtype=jnp.float32) / np.sqrt(fan_in).astype(np.float32)
        inp = {'x': jax.random.normal(ks[0], (B, S, d), dtype=jnp.float32)}
        cn_dims = [(d, d), (d, d // 2), (d // 2, d // 4), (d // 4, 1)]
        for i, (a, b) in enumerate(cn_dims):
            inp[f'cn_w{i + 1}'] = w(ks[1 + i], a, b)
            inp[f'cn_b{i + 1}'] = jnp.zeros((b,), dtype=jnp.float32)
        gc_dims = [(d, d // 2), (d // 2, d // 4), (d // 4, 1)]
        for i, (a, b) in enumerate(gc_dims):
            inp[f'gc_w{i + 1}'] = w(ks[5 + i], a, b)
            inp[f'gc_b{i + 1}'] = jnp.zeros((b,), dtype=jnp.float32)
        inp['adaptive_range'] = jnp.full((1,), 0.2, dtype=jnp.float32)
        return inp
    _L0_ffn_in = _L0_ffn_setup()
    _d = {'L0_attn_resid': _L0_attn_in['resid'], 'L0_attn_norm_w': _L0_attn_in['norm_w'], 'L0_attn_skip_w': _L0_attn_in['skip_w'], 'L0_attn_in_w': _L0_attn_in['in_w'], 'L0_attn_conv_w': _L0_attn_in['conv_w'], 'L0_attn_conv_b': _L0_attn_in['conv_b'], 'L0_attn_wd1': _L0_attn_in['wd1'], 'L0_attn_wd2': _L0_attn_in['wd2'], 'L0_attn_wd2_b': _L0_attn_in['wd2_b'], 'L0_attn_wB': _L0_attn_in['wB'], 'L0_attn_wC': _L0_attn_in['wC'], 'L0_attn_A_log': _L0_attn_in['A_log'], 'L0_attn_W_D': _L0_attn_in['W_D'], 'L0_attn_out_w': _L0_attn_in['out_w'], 'L0_ffn_cn_w1': _L0_ffn_in['cn_w1'], 'L0_ffn_cn_b1': _L0_ffn_in['cn_b1'], 'L0_ffn_cn_w2': _L0_ffn_in['cn_w2'], 'L0_ffn_cn_b2': _L0_ffn_in['cn_b2'], 'L0_ffn_cn_w3': _L0_ffn_in['cn_w3'], 'L0_ffn_cn_b3': _L0_ffn_in['cn_b3'], 'L0_ffn_cn_w4': _L0_ffn_in['cn_w4'], 'L0_ffn_cn_b4': _L0_ffn_in['cn_b4'], 'L0_ffn_gc_w1': _L0_ffn_in['gc_w1'], 'L0_ffn_gc_b1': _L0_ffn_in['gc_b1'], 'L0_ffn_gc_w2': _L0_ffn_in['gc_w2'], 'L0_ffn_gc_b2': _L0_ffn_in['gc_b2'], 'L0_ffn_gc_w3': _L0_ffn_in['gc_w3'], 'L0_ffn_gc_b3': _L0_ffn_in['gc_b3'], 'L0_ffn_adaptive_range': _L0_ffn_in['adaptive_range']}
    _x0 = _d['L0_attn_resid']
    _d['L0_attn_resid'] = jax.random.normal(jax.random.fold_in(jax.random.key(seed), 1), (4, 1024, 256), dtype=_x0.dtype)
    del _x0
    return _d

def reference(L0_attn_resid, L0_attn_norm_w, L0_attn_skip_w, L0_attn_in_w, L0_attn_conv_w, L0_attn_conv_b, L0_attn_wd1, L0_attn_wd2, L0_attn_wd2_b, L0_attn_wB, L0_attn_wC, L0_attn_A_log, L0_attn_W_D, L0_attn_out_w, L0_ffn_cn_w1, L0_ffn_cn_b1, L0_ffn_cn_w2, L0_ffn_cn_b2, L0_ffn_cn_w3, L0_ffn_cn_b3, L0_ffn_cn_w4, L0_ffn_cn_b4, L0_ffn_gc_w1, L0_ffn_gc_b1, L0_ffn_gc_w2, L0_ffn_gc_b2, L0_ffn_gc_w3, L0_ffn_gc_b3, L0_ffn_adaptive_range):

    def _L0_attn_ref(resid, norm_w, skip_w, in_w, conv_w, conv_b, wd1, wd2, wd2_b, wB, wC, A_log, W_D, out_w):
        import jax, jax.numpy as jnp
        import numpy as np
        B_, L_, D_, E_, N_, DR_, DC_ = (2, 512, 256, 512, 16, 64, 4)
        eps = 1e-05
        xn = resid * jax.lax.rsqrt(jnp.mean(resid * resid, axis=-1, keepdims=True) + eps) * norm_w
        skip = jnp.einsum('bld,ed->ble', xn, skip_w)
        x = jnp.einsum('bld,ed->ble', xn, in_w)
        Dc = conv_w.shape[1]
        L = x.shape[1]
        xp = jnp.pad(x, ((0, 0), (Dc - 1, 0), (0, 0)))
        xc = conv_b + sum((xp[:, k:k + L, :] * conv_w[:, k] for k in range(Dc)))
        x = jax.nn.silu(xc)
        delta = jax.nn.softplus(jnp.einsum('blr,er->ble', jnp.einsum('ble,re->blr', x, wd1), wd2) + wd2_b)
        Bm = jnp.einsum('ble,ne->bln', x, wB)
        Cm = jnp.einsum('ble,ne->bln', x, wC)
        A = -jnp.exp(A_log)

        def step(h, inp):
            xt, dt, bt, ct = inp
            h = jnp.exp(dt[:, :, None] * A) * h + (dt * xt)[:, :, None] * bt[:, None, :]
            y = jnp.einsum('ben,bn->be', h, ct)
            return (h, y)
        h0 = jnp.zeros((x.shape[0], A.shape[0], A.shape[1]), x.dtype)
        xs = (jnp.swapaxes(x, 0, 1), jnp.swapaxes(delta, 0, 1), jnp.swapaxes(Bm, 0, 1), jnp.swapaxes(Cm, 0, 1))
        _, ys = jax.lax.scan(step, h0, xs)
        y = jnp.swapaxes(ys, 0, 1) + W_D * x
        y = y * jax.nn.silu(skip)
        out = jnp.einsum('ble,de->bld', y, out_w)
        return resid + out

    def _L0_ffn_ref(x, cn_w1, cn_b1, cn_w2, cn_b2, cn_w3, cn_b3, cn_w4, cn_b4, gc_w1, gc_b1, gc_w2, gc_b2, gc_w3, gc_b3, adaptive_range):
        import jax, jax.numpy as jnp
        import numpy as np
        B, S, DIM = (4, 1024, 256)
        BASE_COUPLING = 0.1
        NUM_CYCLES = 3

        def _gelu(x):
            return jax.nn.gelu(x, approximate=False)

        def _coupling_net(h, w1, b1, w2, b2, w3, b3, w4, b4):
            h = _gelu(h @ w1 + b1)
            h = _gelu(h @ w2 + b2)
            h = _gelu(h @ w3 + b3)
            return jax.nn.sigmoid(h @ w4 + b4)

        def _global_net(h, w1, b1, w2, b2, w3, b3):
            h = _gelu(h @ w1 + b1)
            h = _gelu(h @ w2 + b2)
            return jax.nn.sigmoid(h @ w3 + b3)

        def _twist(x):
            o_r, o_i, p_r, p_i = jnp.split(x, 4, axis=-1)
            return jnp.concatenate([p_r, -p_i, -o_r, o_i], axis=-1)
        global_context = x.mean(axis=1, keepdims=True)
        gf = _global_net(global_context, gc_w1, gc_b1, gc_w2, gc_b2, gc_w3, gc_b3)
        out = x
        for _ in range(NUM_CYCLES):
            tf = _coupling_net(out, cn_w1, cn_b1, cn_w2, cn_b2, cn_w3, cn_b3, cn_w4, cn_b4)
            combined = 0.7 * gf + 0.3 * tf
            coupling = BASE_COUPLING + adaptive_range * (combined - 0.5) * 2.0
            out = out + coupling * _twist(out)
        return out
    x = L0_attn_resid
    x = x + 0.5 * _L0_ffn_ref(_layernorm(x, axis=-1), L0_ffn_cn_w1, L0_ffn_cn_b1, L0_ffn_cn_w2, L0_ffn_cn_b2, L0_ffn_cn_w3, L0_ffn_cn_b3, L0_ffn_cn_w4, L0_ffn_cn_b4, L0_ffn_gc_w1, L0_ffn_gc_b1, L0_ffn_gc_w2, L0_ffn_gc_b2, L0_ffn_gc_w3, L0_ffn_gc_b3, L0_ffn_adaptive_range)
    x = x + _L0_attn_ref(_layernorm(x, axis=-1), L0_attn_norm_w, L0_attn_skip_w, L0_attn_in_w, L0_attn_conv_w, L0_attn_conv_b, L0_attn_wd1, L0_attn_wd2, L0_attn_wd2_b, L0_attn_wB, L0_attn_wC, L0_attn_A_log, L0_attn_W_D, L0_attn_out_w)
    x = x + 0.5 * _L0_ffn_ref(_layernorm(x, axis=-1), L0_ffn_cn_w1, L0_ffn_cn_b1, L0_ffn_cn_w2, L0_ffn_cn_b2, L0_ffn_cn_w3, L0_ffn_cn_b3, L0_ffn_cn_w4, L0_ffn_cn_b4, L0_ffn_gc_w1, L0_ffn_gc_b1, L0_ffn_gc_w2, L0_ffn_gc_b2, L0_ffn_gc_w3, L0_ffn_gc_b3, L0_ffn_adaptive_range)
    return x

_drawn_inputs = setup_inputs


def setup_inputs(seed=0):
    import zlib

    import numpy as np

    out = dict(_drawn_inputs(seed))
    spreads = {'L0_attn_norm_w': (1.0, 0.2),
     'L0_attn_W_D': (1.0, 0.2),
     'L0_ffn_cn_b1': (0.0, 0.8),
     'L0_ffn_cn_b2': (0.0, 0.8),
     'L0_ffn_cn_b3': (0.0, 0.8),
     'L0_ffn_gc_b1': (0.0, 0.8),
     'L0_ffn_gc_b2': (0.0, 0.8)}
    factors = {'L0_attn_conv_b': 3.39,
     'L0_attn_wd1': 8.0,
     'L0_attn_wd2': 8.0,
     'L0_attn_wd2_b': 5.92,
     'L0_attn_wB': 3.635,
     'L0_attn_wC': 3.919,
     'L0_attn_A_log': 6.748,
     'L0_ffn_cn_w1': 7.502,
     'L0_ffn_cn_w2': 7.868,
     'L0_ffn_cn_w3': 6.311,
     'L0_ffn_cn_w4': 7.012,
     'L0_ffn_gc_w1': 8.0,
     'L0_ffn_gc_w2': 8.0,
     'L0_ffn_gc_w3': 5.693}
    for name, (base, spread) in spreads.items():
        noise = np.random.default_rng([zlib.crc32(name.encode()), seed]).standard_normal(out[name].shape)
        drawn = base * np.exp(spread * noise) if base else spread * noise
        out[name] = jnp.asarray(drawn.astype(out[name].dtype))
    for name, factor in factors.items():
        out[name] = (out[name] * factor).astype(out[name].dtype)
    return out
```

```python
from contextlib import ExitStack

import concourse.bass as bass
from concourse import mybir

F32 = mybir.dt.float32
BF16 = mybir.dt.bfloat16
ALU = mybir.AluOpType
ACT = mybir.ActivationFunctionType
AX = mybir.AxisListType

P = 128
BATCH, SEQ, DIM = 4, 1024, 256
INNER, STATE, RANK, TAPS = 512, 16, 64, 4
EPS = 1e-5
KD = DIM // P
KE = INNER // P
TILES = BATCH * SEQ // P
BT = SEQ // P
BANK = 512
HALVES = SEQ // BANK
XROWS = RANK + 2 * STATE
H3 = 64
CYCLES = 3

W256 = {"in": (0, INNER), "skip": (INNER, INNER), "w1": (2 * INNER, DIM), "w2": (2 * INNER + DIM, P),
        "g1": (2 * INNER + DIM + P, P)}
W256_COLS = 2 * INNER + DIM + 2 * P
W512 = {"xproj": (0, XROWS), "out": (XROWS, DIM), "conv": (XROWS + DIM, TAPS)}
_o = XROWS + DIM + TAPS
W512.update({"conv_b": (_o, 1), "D": (_o + 1, 1), "dt_b": (_o + 2, 1), "A_log": (_o + 3, STATE)})
W512_COLS = _o + 3 + STATE
W128 = {"w3": (0, H3), "g2": (H3, H3), "w4": (2 * H3, P)}
_o = 2 * H3 + P
for _n, _w in (("b2", 1), ("gb1", 1), ("norm", KD), ("b1", KD), ("b3", 1), ("b4", 1), ("gb3", 1), ("ar", 1)):
    W128[_n] = (_o, _w)
    _o += _w
W128_COLS = _o
W64 = {"dt": (0, INNER), "g3": (INNER, P), "gb2": (INNER + P, 1)}
W64_COLS = INNER + P + 1


class Chain:

    def __init__(self, engine, sem, per_turn=0, turn=0):
        self.engine, self.sem, self.count, self.per_turn, self.turn = engine, sem, 0, per_turn, turn

    def __call__(self, instruction):
        self.count += 1
        instruction.then_inc(self.sem, 1)
        self.engine.wait_ge(self.sem, self.turn * self.per_turn + self.count)

    def end(self):
        assert self.count == self.per_turn, self.count


def ffn(nc, sems, mem, name, load_sem, store):
    GROUP = 2
    TURNS = BATCH // GROUP
    GT = GROUP * BT
    STEPS = CYCLES * GROUP
    VEC_CHAIN = 1 + 1 + 3
    x_tok, w256, w128, w64 = mem["x_tok"], mem["w256"], mem["w128"], mem["w64"]
    ident, sign = mem["ident"], mem["sign"]
    with ExitStack() as ctx:
        sb = lambda n, s, d=F32: ctx.enter_context(nc.sbuf_tensor(f"{name}_{n}", s, d))
        sem = lambda n: ctx.enter_context(nc.semaphore(f"{name}_{n}"))
        bank = [ctx.enter_context(nc.psum_tensor(f"{name}_bank{i}", [P, BANK], F32)) for i in range(8)]
        stats = sb("stats", [P, GT, 6])
        scratch = sb("scratch", [P, 1])
        moments = sb("moments", [P, GT, 2])
        std = sb("std", [P, GT])
        rstd = sb("rstd", [P, GT])
        z_tok = sb("z_tok", [P, 4, DIM])
        state = sb("state", [P, KD, GROUP * SEQ])
        total = sb("total", [P, KD, GROUP])
        g1 = sb("g1", [P, GROUP])
        g2 = sb("g2", [H3, GROUP])
        gt = sb("gt", [P, GROUP])
        base = sb("base", [P, GROUP])
        slope = sb("slope", [P, 1])
        half_b4 = sb("half_b4", [P, 2])
        h1 = sb("h1", [P, KD, SEQ])
        h2 = sb("h2", [P, SEQ])
        h3 = sb("h3", [P, BANK])
        th = sb("th", [P, SEQ])
        couple = sb("couple", [P, SEQ])
        turned = sb("turned", [P, KD, SEQ])

        moments_ready, std_ready, z_ready = sem("moments"), sem("std"), sem("z")
        tr_ready, state_in, total_ready = sem("tr"), sem("state_in"), sem("total")
        pe_g, act_g, base_ready = sem("pe_g"), sem("act_g"), sem("base")
        l1_done, l2_done, l3_done, l4_done = sem("l1"), sem("l2"), sem("l3"), sem("l4")
        h1_ready, h2_ready, h3_ready, th_ready = sem("h1r"), sem("h2r"), sem("h3r"), sem("thr")
        updated, back_ready, back_added = sem("updated"), sem("back"), sem("added")
        vec, vec2, stored = sem("vec"), sem("vec2"), sem("stored")
        block = ctx.enter_context(nc.Block())

        def w(t, table, key, k=None):
            o, n = table[key]
            return t[:, k, o:o + n] if k is not None else t[:, o:o + n]

        @block.vector
        def _(dve):
            if load_sem is not None:
                dve.wait_ge(load_sem["weights"], 64)
            nc.vector.tensor_scalar(half_b4[:, 0:1], w(w128, W128, "b4"), 0.5, None, ALU.mult)
            nc.vector.tensor_scalar(half_b4[:, 1:2], w(w128, W128, "gb3"), 0.5, None, ALU.mult)
            nc.vector.tensor_scalar(slope[:, :], w(w128, W128, "ar"), sign[:, 0:1], 0.3, ALU.mult, ALU.mult)\
                .then_inc(vec2, 1)
            with dve.Fori(0, TURNS) as g:
                chain = Chain(dve, vec, VEC_CHAIN, g)
                for t in range(GT):
                    if load_sem is not None and t % BT == 0:
                        dve.wait_ge(load_sem["x"], g * GROUP + t // BT + 1)
                    last = nc.vector.bn_stats(stats[:, t, :], x_tok[:, g * GT + t, :])
                chain(last)
                nc.vector.memset(scratch[:, :], 0.0)
                for t in range(GT):
                    last = nc.vector.bn_aggr(moments[:, t, :], stats[:, t, :])
                last.then_inc(moments_ready, 1)
                dve.wait_ge(std_ready, g + 1)
                chain(nc.vector.reciprocal(rstd[:, :], std[:, :]))
                for t in range(GT):
                    if t >= 4:
                        dve.wait_ge(tr_ready, g * GT + t - 3)
                    nc.vector.tensor_scalar(z_tok[:, t % 4, :], x_tok[:, g * GT + t, :], moments[:, t, 0:1],
                                            rstd[:, t:t + 1], ALU.subtract, ALU.mult).then_inc(z_ready, 1)
                dve.wait_ge(state_in, (g + 1) * GT // 2)
                nc.vector.tensor_reduce(total[:, :, :], state[:, :, :].rearrange("p k (b n) -> p k b n", b=GROUP),
                                        AX.X, ALU.add).then_inc(total_ready, 1)
                dve.wait_ge(act_g, (g + 1) * 3)
                chain(nc.vector.tensor_scalar(base[:, :], gt[:, :], w(w128, W128, "ar"), 0.7, ALU.mult, ALU.mult))
                chain(nc.vector.tensor_scalar(gt[:, :], base[:, :], 0.1, None, ALU.add))
                chain(nc.vector.tensor_scalar(base[:, :], gt[:, :], sign[:, 0:1], None, ALU.mult))
                chain.end()
                steps = Chain(dve, updated, STEPS * HALVES * 5, g)
                for s in range(STEPS):
                    b = s % GROUP
                    for h in range(HALVES):
                        c = slice(h * BANK, (h + 1) * BANK)
                        cs = slice(b * SEQ + h * BANK, b * SEQ + (h + 1) * BANK)
                        dve.wait_ge(th_ready, (g * STEPS + s) * HALVES + h + 1)
                        steps(nc.vector.tensor_scalar(couple[:, c], th[:, c], slope[:, 0:1], base[:, b:b + 1],
                                                      ALU.mult, ALU.add))
                        nc.vector.tensor_tensor(turned[:, 0, c], couple[:, c], state[:, 1, cs], ALU.mult)\
                            .then_inc(updated, 1)
                        nc.vector.tensor_tensor(turned[:, 1, c], couple[:, c], state[:, 0, cs], ALU.mult)\
                            .then_inc(updated, 1)
                        steps.count += 2
                        dve.wait_ge(updated, g * steps.per_turn + steps.count)
                        nc.vector.tensor_tensor(state[:, 0, cs], state[:, 0, cs], turned[:, 0, c], ALU.add)\
                            .then_inc(updated, 1)
                        nc.vector.tensor_tensor(state[:, 1, cs], state[:, 1, cs], turned[:, 1, c], ALU.subtract)\
                            .then_inc(updated, 1)
                        steps.count += 2
                steps.end()
                for t in range(GT // 2):
                    dve.wait_ge(back_ready, g * (GT // 2) + t + 1)
                    nc.vector.scalar_tensor_tensor(
                        x_tok[:, bass.ds(g * GT + 2 * t, 2), :],
                        bank[t % 4][:, :].rearrange("p (a d) -> p a d", a=2), 0.5,
                        x_tok[:, bass.ds(g * GT + 2 * t, 2), :], ALU.mult, ALU.add).then_inc(back_added, 1)

        @block.tensor
        def _(pe):
            if load_sem is not None:
                pe.wait_ge(load_sem["weights"], 64)
                pe.wait_ge(load_sem["ident"], 2)
            with pe.Fori(0, TURNS) as g:
                for t in range(GT):
                    if t % 2 == 0 and t >= 8:
                        pe.wait_ge(state_in, g * (GT // 2) + t // 2 - 3)
                    pe.wait_ge(z_ready, g * GT + t + 1)
                    for k in range(KD):
                        o = (2 * k + t % 2) * P
                        last = nc.tensor.transpose(bank[t // 2 % 4][:, o:o + P], z_tok[:, t % 4, k * P:(k + 1) * P],
                                                   ident[:, :])
                    last.then_inc(tr_ready, 1)
                pe.wait_ge(total_ready, g + 1)
                for k in range(KD):
                    last = nc.tensor.matmul(bank[7][:, 0:GROUP], w(w256, W256, "g1", k), total[:, k, :],
                                            start=k == 0, stop=k == KD - 1)
                last.then_inc(pe_g, 1)
                pe.wait_ge(act_g, g * 3 + 1)
                nc.tensor.matmul(bank[6][0:H3, 0:GROUP], w(w128, W128, "g2"), g1[:, :], start=True, stop=True)\
                    .then_inc(pe_g, 1)
                pe.wait_ge(act_g, g * 3 + 2)
                nc.tensor.matmul(bank[5][:, 0:GROUP], w(w64, W64, "g3"), g2[:, :], start=True, stop=True)\
                    .then_inc(pe_g, 1)

                def layer1(s, h, m):
                    b = s % GROUP
                    if s > 0:
                        pe.wait_ge(h1_ready, (g * STEPS + s - 1) * 4 + h * 2 + m + 1)
                    else:
                        pe.wait_ge(state_in, (g + 1) * (GT // 2))
                    if s >= GROUP:
                        pe.wait_ge(updated, g * STEPS * HALVES * 5 + ((s - GROUP) * HALVES + h + 1) * 5)
                    for k in range(KD):
                        o = W256["w1"][0] + m * P
                        last = nc.tensor.matmul(bank[h * 2 + m][:, :], w256[:, k, o:o + P],
                                                state[:, k, b * SEQ + h * BANK:b * SEQ + (h + 1) * BANK],
                                                start=k == 0, stop=k == KD - 1)
                    last.then_inc(l1_done, 1)

                def layer2(s, h):
                    pe.wait_ge(h1_ready, (g * STEPS + s) * 4 + h * 2 + 2)
                    if s > 0 and h == 0:
                        pe.wait_ge(th_ready, (g * STEPS + s) * HALVES)
                    if s > 0 and h == 1:
                        pe.wait_ge(h2_ready, (g * STEPS + s) * HALVES)
                    for k in range(KD):
                        last = nc.tensor.matmul(bank[4 + h][:, :], w(w256, W256, "w2", k),
                                                h1[:, k, h * BANK:(h + 1) * BANK], start=k == 0, stop=k == KD - 1)
                    last.then_inc(l2_done, 1)

                def layer3(s):
                    pe.wait_ge(h2_ready, (g * STEPS + s) * HALVES + 2)
                    for h in range(HALVES):
                        last = nc.tensor.matmul(bank[6][h * H3:(h + 1) * H3, :], w(w128, W128, "w3"),
                                                h2[:, h * BANK:(h + 1) * BANK], start=True, stop=True)
                    last.then_inc(l3_done, 1)

                def layer4(s):
                    pe.wait_ge(h3_ready, g * STEPS + s + 1)
                    for h in range(HALVES):
                        o = W128["w4"][0]
                        last = nc.tensor.matmul(bank[7 if h == 0 else 4][:, :],
                                                w128[h * H3:(h + 1) * H3, o:o + P],
                                                h3[h * H3:(h + 1) * H3, :], start=True, stop=True)
                    last.then_inc(l4_done, 1)

                pe.wait_ge(act_g, g * 3 + 3)
                for s in range(STEPS + 1):
                    if s < STEPS:
                        layer1(s, 0, 0)
                    if s > 0:
                        layer3(s - 1)
                    if s < STEPS:
                        layer1(s, 0, 1)
                    if s > 0:
                        layer4(s - 1)
                    if s < STEPS:
                        layer1(s, 1, 0)
                        layer1(s, 1, 1)
                        layer2(s, 0)
                        layer2(s, 1)
                for t in range(GT):
                    if t % 2 == 0:
                        if t >= 8:
                            pe.wait_ge(back_added, g * (GT // 2) + t // 2 - 3)
                        b, h = t // BT, t % BT * P // BANK
                        pe.wait_ge(updated, g * STEPS * HALVES * 5 + ((STEPS - GROUP + b) * HALVES + h + 1) * 5)
                    for k in range(KD):
                        o = (t % 2) * DIM + k * P
                        last = nc.tensor.transpose(bank[t // 2 % 4][:, o:o + P], state[:, k, t * P:(t + 1) * P],
                                                   ident[:, :])
                    if t % 2:
                        last.then_inc(back_ready, 1)
                pe.wait_ge(back_added, (g + 1) * (GT // 2))

        @block.scalar
        def _(act):
            if load_sem is not None:
                act.wait_ge(load_sem["weights"], 64)
            act.wait_ge(vec2, 1)
            with act.Fori(0, TURNS) as g:
                act.wait_ge(moments_ready, g + 1)
                nc.scalar.activation(std[:, :], moments[:, :, 1], ACT.Sqrt, bias=mem["eps"][:, 0:1])\
                    .then_inc(std_ready, 1)
                for t in range(GT // 2):
                    act.wait_ge(tr_ready, g * GT + 2 * t + 2)
                    nc.scalar.activation(state[:, :, 2 * t * P:2 * (t + 1) * P],
                                         bank[t % 4][:, :].rearrange("p (k n) -> p k n", k=KD),
                                         ACT.Copy).then_inc(state_in, 1)
                act.wait_ge(pe_g, g * 3 + 1)
                nc.scalar.activation(g1[:, :], bank[7][:, 0:GROUP], ACT.Gelu, bias=w(w128, W128, "gb1"),
                                     scale=1.0 / SEQ).then_inc(act_g, 1)
                act.wait_ge(pe_g, g * 3 + 2)
                nc.scalar.activation(g2[:, :], bank[6][0:H3, 0:GROUP], ACT.Gelu, bias=w64[:, W64["gb2"][0]:][:, 0:1])\
                    .then_inc(act_g, 1)
                act.wait_ge(pe_g, g * 3 + 3)
                nc.scalar.activation(gt[:, :], bank[5][:, 0:GROUP], ACT.Tanh, bias=half_b4[:, 1:2], scale=0.5)\
                    .then_inc(act_g, 1)

                def gelu1(s, h, m):
                    act.wait_ge(l1_done, (g * STEPS + s) * 4 + h * 2 + m + 1)
                    o = W128["b1"][0] + m
                    nc.scalar.activation(h1[:, m, h * BANK:(h + 1) * BANK], bank[h * 2 + m][:, :], ACT.Gelu,
                                         bias=w128[:, o:o + 1]).then_inc(h1_ready, 1)

                def gelu2(s, h):
                    act.wait_ge(l2_done, (g * STEPS + s) * HALVES + h + 1)
                    nc.scalar.activation(h2[:, h * BANK:(h + 1) * BANK], bank[4 + h][:, :], ACT.Gelu,
                                         bias=w(w128, W128, "b2")).then_inc(h2_ready, 1)

                def gelu3(s):
                    act.wait_ge(l3_done, g * STEPS + s + 1)
                    nc.scalar.activation(h3[:, :], bank[6][:, :], ACT.Gelu, bias=w(w128, W128, "b3"))\
                        .then_inc(h3_ready, 1)

                def tanh4(s, h):
                    act.wait_ge(l4_done, g * STEPS + s + 1)
                    if s > 0:
                        act.wait_ge(updated, g * STEPS * HALVES * 5 + ((s - 1) * HALVES + h + 1) * 5)
                    nc.scalar.activation(th[:, h * BANK:(h + 1) * BANK], bank[7 if h == 0 else 4][:, :], ACT.Tanh,
                                         bias=half_b4[:, 0:1], scale=0.5).then_inc(th_ready, 1)

                for s in range(STEPS + 1):
                    if s < STEPS:
                        gelu1(s, 0, 0)
                    if s > 0:
                        gelu3(s - 1)
                    if s < STEPS:
                        gelu1(s, 0, 1)
                    if s > 0:
                        tanh4(s - 1, 0)
                        tanh4(s - 1, 1)
                    if s < STEPS:
                        gelu1(s, 1, 0)
                        gelu1(s, 1, 1)
                        gelu2(s, 0)
                        gelu2(s, 1)

        if load_sem is not None:
            @block.sync
            def _(sp):
                for b in range(BATCH):
                    sp.wait_ge(load_sem[f"x{b}"], 16)
                    sp.sem_inc(load_sem["x"], 1)

        if store is not None:
            @block.sync
            def _(sp):
                with sp.Fori(0, TURNS) as g:
                    sp.wait_ge(back_added, (g + 1) * (GT // 2))
                    sp.dma_start(store[:, bass.ds(g * GT, GT), :], x_tok[:, bass.ds(g * GT, GT), :])\
                        .then_inc(stored, 16)
                sp.wait_ge(stored, TURNS * 16)


def setup(nc, mem, load_sem, ins):
    x_tok = mem["x_tok"]
    with nc.Block() as block:
        @block.sync
        def _(sp):
            for b in range(BATCH):
                sp.dma_start(x_tok[:, b * BT:(b + 1) * BT, :], ins["x"][:, b * BT:(b + 1) * BT, :])\
                    .then_inc(load_sem[f"x{b}"], 16)

        @block.scalar
        def _(act):
            for n in ("w256", "w128", "w64", "w512"):
                act.dma_start(mem[n][...], ins[n]).then_inc(load_sem["weights"], 16)

        @block.vector
        def _(dve):
            nc.vector.memset(mem["eps"][:, :], EPS)
            nc.vector.memset(mem["sign"][0:H3, :], 1.0)
            nc.vector.memset(mem["sign"][H3:P, :], -1.0)

        @block.gpsimd
        def _(pool):
            nc.gpsimd.memset(mem["ident"][:, :], 0.0).then_inc(load_sem["ident"], 1)
            nc.gpsimd.memset(mem["select"][:, :, :], 0.0).then_inc(load_sem["select"], 1)
            pool.wait_ge(load_sem["ident"], 1)
            nc.gpsimd.affine_select(out=mem["ident"][:, :], in_=mem["ident"][:, :], compare_op=ALU.not_equal,
                                    fill=1.0, base=0, pattern=[[-1, P]], channel_multiplier=1)\
                .then_inc(load_sem["ident"], 1)
            for a in range(3):
                pool.wait_ge(load_sem["select"], a + 1)
                nc.gpsimd.affine_select(out=mem["select"][:, :, :], in_=mem["select"][:, :, :],
                                        compare_op=ALU.not_equal, fill=1.0, base=-32 * a,
                                        pattern=[[-1, 2 * STATE], [0, P]], channel_multiplier=1)\
                    .then_inc(load_sem["select"], 1)


def mamba(nc, mem):
    x_tok, w256, w512, w64, w128 = mem["x_tok"], mem["w256"], mem["w512"], mem["w64"], mem["w128"]
    ident, select, eps = mem["ident"], mem["select"], mem["eps"]
    HT = BANK // P
    with ExitStack() as ctx:
        sb = lambda n, s, d=F32: ctx.enter_context(nc.sbuf_tensor(f"m_{n}", s, d))
        sem = lambda n: ctx.enter_context(nc.semaphore(f"m_{n}"))
        bank = [ctx.enter_context(nc.psum_tensor(f"m_bank{i}", [P, BANK], F32)) for i in range(8)]
        stats = sb("stats", [P, BT, 6])
        scratch = sb("scratch", [P, 1])
        moments = sb("moments", [P, BT, 2])
        root = sb("root", [P, 2, BT])
        inverse = sb("inverse", [P, 2, BT])
        square = sb("square", [P, 2, BT])
        z_tok = sb("z_tok", [P, 2, DIM])
        xn_tok = sb("xn_tok", [P, 2, DIM])
        xn = sb("xn", [P, KD, SEQ])
        negA = sb("negA", [P, KE, STATE])
        expA = sb("expA", [P, KE, STATE])
        conv = sb("conv", [P, KE, TAPS + 1])
        pre = sb("pre", [P, KE, TAPS - 1 + BANK])
        acc = sb("acc", [P, 2, BANK])
        th = sb("th", [P, 2, BANK])
        gate = sb("gate", [P, KE, BANK])
        x = sb("x", [P, KE, BANK])
        rank = sb("rank", [RANK, BANK])
        part = sb("part", [96, BANK])
        mid = sb("mid", [96, BANK], BF16)
        parts = sb("parts", [96, BANK], BF16)
        delta = sb("delta", [P, KE, BANK])
        dx = sb("dx", [P, KE, BANK])
        brow = sb("brow", [P, 2, BANK])
        u = sb("u", [P, 2, KE, BANK])
        hid = sb("hid", [P, 2, KE, BANK])
        carry = sb("carry", [P, STATE, KE])
        hc = sb("hc", [P, 2, KE, BANK])
        y = hid
        v, e, u1, ln = hc[:, 0], hc[:, 1], hid[:, 0], hid[:, 1]

        load = {n: sem(n) for n in (
            "negA", "moments", "inv", "root", "xn_ready", "tr", "xn_in", "skip_done", "in_done", "tanh_g",
            "gate", "pre", "conv", "tanh_x", "x", "xproj", "parts", "rank", "dt_done", "v", "e", "u1", "ln", "delta", "abs", "carry",
            "dx", "b_done", "c_done", "brow", "u", "a", "scan", "hc", "y_part", "y", "out", "added", "pool", "dve",
            "actc")}
        S = load
        block = ctx.enter_context(nc.Block())
        N = STATE

        def col(key, c, n=1):
            o = W512[key][0]
            return w512[:, c, o:o + n]

        CH = 4 + 3 * BT + HALVES * (KE * 3 + 4 + 2 + KE + 1)

        @block.scalar
        def _(act):
            actc = Chain(act, S["actc"])
            o = W512["A_log"][0]
            actc(nc.scalar.activation(expA[:, :, :], w512[:, :, o:o + STATE], ACT.Exp))
            nc.scalar.mul(negA[:, :, :], expA[:, :, :], -1.0).then_inc(S["negA"], 1)
            act.wait_ge(S["negA"], 1)
            with act.Fori(0, BATCH) as b:
                act.wait_ge(S["moments"], 2 * b + 1)
                nc.scalar.activation(root[:, 0, :], moments[:, :, 1], ACT.Sqrt, bias=eps[:, 0:1]).then_inc(S["root"], 1)
                act.wait_ge(S["moments"], 2 * b + 2)
                nc.scalar.activation(root[:, 1, :], square[:, 1, :], ACT.Sqrt, bias=eps[:, 0:1]).then_inc(S["root"], 1)
                for t in range(BT):
                    act.wait_ge(S["tr"], b * BT + t + 1)
                    for k in range(KD):
                        o = W128["norm"][0] + k
                        last = nc.scalar.activation(xn[:, k, t * P:(t + 1) * P],
                                                    bank[t % 4][:, k * P:(k + 1) * P], ACT.Copy,
                                                    scale=w128[:, o:o + 1])
                    last.then_inc(S["xn_in"], 1)
                for h in range(HALVES):
                    i = b * HALVES + h
                    for c in range(KE):
                        act.wait_ge(S["skip_done"], i * KE + c + 1)
                        if c >= 2:
                            act.wait_ge(S["gate"], i * KE + c - 1)
                        nc.scalar.activation(th[:, c % 2, :], bank[c % 2][:, :], ACT.Tanh, scale=0.5)\
                            .then_inc(S["tanh_g"], 1)
                    for c in range(KE):
                        act.wait_ge(S["in_done"], i * KE + c + 1)
                        nc.scalar.activation(pre[:, c, TAPS - 1:TAPS - 1 + BANK], bank[2 + c % 2][:, :], ACT.Copy)\
                            .then_inc(S["pre"], 1)
                    for c in range(KE):
                        act.wait_ge(S["conv"], i * KE + c + 1)
                        nc.scalar.activation(th[:, c % 2, :], acc[:, c % 2, :], ACT.Tanh).then_inc(S["tanh_x"], 1)
                    act.wait_ge(S["xproj"], i + 1)
                    nc.scalar.activation(rank[:, :], bank[4][0:RANK, :], ACT.Copy).then_inc(S["rank"], 1)
                    for c in range(KE):
                        act.wait_ge(S["dt_done"], i * KE + c + 1)
                        nc.scalar.activation(v[:, c, :], bank[c][:, :], ACT.Identity, bias=col("dt_b", c))\
                            .then_inc(S["v"], 1)
                    act.wait_ge(S["v"], (i + 1) * KE)
                    nc.scalar.activation(ln[:, :, :], v[:, :, :], ACT.Abs).then_inc(S["abs"], 1)
                    act.wait_ge(S["abs"], i + 1)
                    nc.scalar.activation(e[:, :, :], ln[:, :, :], ACT.Exp, scale=-1.0).then_inc(S["e"], 1)
                    act.wait_ge(S["u1"], i + 1)
                    nc.scalar.activation(ln[:, :, :], u1[:, :, :], ACT.Ln).then_inc(S["ln"], 1)
                    act.wait_ge(S["delta"], i + 1)
                    for n in range(N):
                        j = i * N + n
                        act.wait_ge(S["b_done"], j + 1)
                        if n >= 2:
                            act.wait_ge(S["u"], j - 1)
                        nc.scalar.activation(brow[:, n % 2, :], bank[6][:, :], ACT.Copy).then_inc(S["brow"], 1)
                        for c in range(KE):
                            if n > 0 or c >= 2:
                                act.wait_ge(S["scan"], j * KE + c - 1)
                            nc.scalar.activation(bank[4 + c % 2][:, :], delta[:, c, :], ACT.Exp,
                                                 scale=negA[:, c, n:n + 1]).then_inc(S["a"], 1)

        @block.gpsimd
        def _(pool):
            with pool.Fori(0, BATCH) as b:
                for h in range(HALVES):
                    i = b * HALVES + h
                    pool.wait_ge(S["delta"], i + 1)
                    nc.gpsimd.tensor_tensor(dx[:, :, :], delta[:, :, :], x[:, :, :], ALU.mult).then_inc(S["dx"], 1)
                    pool.wait_ge(S["dx"], i + 1)
                    for n in range(N):
                        j = i * N + n
                        pool.wait_ge(S["brow"], j + 1)
                        if n >= 2:
                            pool.wait_ge(S["scan"], (j - 1) * KE)
                        nc.gpsimd.tensor_tensor(u[:, n % 2, :, :], dx[:, :, :],
                                                brow[:, n % 2, :].unsqueeze(1).to_broadcast([P, KE, BANK]),
                                                ALU.mult).then_inc(S["u"], 1)

        @block.vector
        def _(dve):
            o = W512["conv"][0]
            nc.vector.tensor_scalar(conv[:, :, :], w512[:, :, o:o + TAPS + 1], 0.5, None, ALU.mult)\
                .then_inc(S["pool"], 1)
            dve.wait_ge(S["pool"], 1)
            with dve.Fori(0, BATCH) as b:
                chain = Chain(dve, S["dve"], CH, b)
                for t in range(BT):
                    last = nc.vector.bn_stats(stats[:, t, :], x_tok[:, b * BT + t, :])
                chain(last)
                nc.vector.memset(scratch[:, :], 0.0)
                for t in range(BT):
                    last = nc.vector.bn_aggr(moments[:, t, :], stats[:, t, :])
                last.then_inc(S["moments"], 1)
                dve.wait_ge(S["root"], 2 * b + 1)
                chain(nc.vector.reciprocal(inverse[:, 0, :], root[:, 0, :]))
                chain(nc.vector.tensor_tensor(square[:, 0, :], inverse[:, 0, :], inverse[:, 0, :], ALU.mult))
                nc.vector.tensor_tensor(square[:, 1, :], square[:, 0, :], moments[:, :, 1], ALU.mult)\
                    .then_inc(S["moments"], 1)
                dve.wait_ge(S["root"], 2 * b + 2)
                chain(nc.vector.reciprocal(inverse[:, 1, :], root[:, 1, :]))
                for t in range(BT):
                    chain(nc.vector.tensor_scalar(z_tok[:, t % 2, :], x_tok[:, b * BT + t, :], moments[:, t, 0:1],
                                                  inverse[:, 0, t:t + 1], ALU.subtract, ALU.mult))
                    if t >= 2:
                        dve.wait_ge(S["tr"], b * BT + t - 1)
                    chain(nc.vector.tensor_scalar(xn_tok[:, t % 2, :], z_tok[:, t % 2, :], inverse[:, 1, t:t + 1],
                                                  None, ALU.mult))
                    chain(nc.vector.tensor_tensor(x_tok[:, b * BT + t, :], x_tok[:, b * BT + t, :],
                                                  z_tok[:, t % 2, :], ALU.add))
                for h in range(HALVES):
                    i = b * HALVES + h
                    for c in range(KE):
                        dve.wait_ge(S["tanh_g"], i * KE + c + 1)
                        nc.vector.scalar_tensor_tensor(gate[:, c, :], th[:, c % 2, :], 1.0, bank[c % 2][:, :],
                                                       ALU.add, ALU.mult).then_inc(S["gate"], 1)
                    if h == 0:
                        chain(nc.vector.memset(pre[:, :, 0:TAPS - 1], 0.0))
                    for c in range(KE):
                        a = acc[:, c % 2, :]
                        dve.wait_ge(S["pre"], i * KE + c + 1)
                        if c >= 2:
                            dve.wait_ge(S["tanh_x"], i * KE + c - 1)
                        chain(nc.vector.tensor_scalar(a, pre[:, c, 0:BANK], conv[:, c, 0:1],
                                                      conv[:, c, TAPS:TAPS + 1], ALU.mult, ALU.add))
                        for k in range(1, TAPS):
                            op = nc.vector.scalar_tensor_tensor(a, pre[:, c, k:k + BANK], conv[:, c, k:k + 1], a,
                                                                ALU.mult, ALU.add)
                            if k < TAPS - 1:
                                chain(op)
                            else:
                                op.then_inc(S["conv"], 1)
                        dve.wait_ge(S["tanh_x"], i * KE + c + 1)
                        nc.vector.scalar_tensor_tensor(x[:, c, :], th[:, c % 2, :], 1.0, a, ALU.add, ALU.mult)\
                            .then_inc(S["x"], 1)
                    if h == 0:
                        chain(nc.vector.tensor_copy(pre[:, :, 0:TAPS - 1], pre[:, :, BANK:BANK + TAPS - 1]))
                    R = slice(RANK, XROWS)
                    dve.wait_ge(S["xproj"], i + 1)
                    dve.wait_ge(S["rank"], i + 1)
                    chain(nc.vector.tensor_copy(parts[R, :], bank[4][R, :]))
                    chain(nc.vector.tensor_tensor(part[R, :], bank[4][R, :], parts[R, :], ALU.subtract))
                    chain(nc.vector.tensor_copy(mid[R, :], part[R, :]))
                    chain(nc.vector.tensor_copy(parts[0:32, :], mid[R, :]))
                    nc.vector.tensor_tensor(parts[32:64, :], part[R, :], mid[R, :], ALU.subtract)\
                        .then_inc(S["parts"], 1)
                    dve.wait_ge(S["e"], i + 1)
                    nc.vector.tensor_scalar(u1[:, :, :], e[:, :, :], 1.0, None, ALU.add).then_inc(S["u1"], 1)
                    dve.wait_ge(S["ln"], i + 1)
                    chain(nc.vector.scalar_tensor_tensor(e[:, :, :], u1[:, :, :], -1.0, e[:, :, :],
                                                         ALU.add, ALU.subtract))
                    chain(nc.vector.tensor_tensor(e[:, :, :], ln[:, :, :], e[:, :, :], ALU.subtract))
                    nc.vector.scalar_tensor_tensor(delta[:, :, :], v[:, :, :], 0.0, e[:, :, :], ALU.max, ALU.add)\
                        .then_inc(S["delta"], 1)
                    if h > 0:
                        dve.wait_ge(S["carry"], (b + 1) * N)
                    for n in range(N + 1):
                        j = i * N + n
                        if n < N:
                            dve.wait_ge(S["u"], j + 1)
                            if n >= 2:
                                dve.wait_ge(S["hc"], j - 1)
                            for c in range(KE):
                                dve.wait_ge(S["a"], j * KE + c + 1)
                                nc.vector.tensor_tensor_scan(
                                    hid[:, n % 2, c, :], bank[4 + c % 2][:, :], u[:, n % 2, c, :],
                                    0.0 if h == 0 else carry[:, n, c:c + 1], ALU.mult, ALU.add)\
                                    .then_inc(S["scan"], 1)
                        if n > 0:
                            m = n - 1
                            dve.wait_ge(S["scan"], j * KE)
                            if h == 0:
                                nc.vector.tensor_copy(carry[:, m, :], hid[:, m % 2, :, BANK - 1])\
                                    .then_inc(S["carry"], 1)
                            dve.wait_ge(S["c_done"], j)
                            if m >= 2:
                                dve.wait_ge(S["y_part"], j - 2)
                            nc.vector.tensor_tensor(hc[:, m % 2, :, :], hid[:, m % 2, :, :],
                                                    bank[7][:, :].unsqueeze(1).to_broadcast([P, KE, BANK]),
                                                    ALU.mult).then_inc(S["hc"], 1)
                    dve.wait_ge(S["y_part"], (i + 1) * N)
                    dve.wait_ge(S["hc"], (i + 1) * N)
                    for c in range(KE):
                        chain(nc.vector.scalar_tensor_tensor(y[:, 0, c, :], x[:, c, :], col("D", c), bank[c][:, :],
                                                             ALU.mult, ALU.add))
                        nc.vector.scalar_tensor_tensor(y[:, 1, c, :], y[:, 0, c, :], 0.5, gate[:, c, :],
                                                       ALU.mult, ALU.mult).then_inc(S["y"], 1)
                    for t in range(HT):
                        dve.wait_ge(S["out"], i * HT + t + 1)
                        at = b * BT + h * HT + t
                        nc.vector.tensor_tensor(x_tok[:, at, :], x_tok[:, at, :], bank[4 + t % 2][:, 0:DIM],
                                                ALU.add).then_inc(S["added"], 1)
                assert chain.count == CH, chain.count

        @block.tensor
        def _(pe):
            with pe.Fori(0, BATCH) as b:
                for t in range(BT):
                    pe.wait_ge(S["dve"], b * CH + 4 + 3 * t + 2)
                    if t >= 4:
                        pe.wait_ge(S["xn_in"], b * BT + t - 3)
                    for k in range(KD):
                        last = nc.tensor.transpose(bank[t % 4][:, k * P:(k + 1) * P],
                                                   xn_tok[:, t % 2, k * P:(k + 1) * P], ident[:, :])
                    last.then_inc(S["tr"], 1)
                pe.wait_ge(S["xn_in"], (b + 1) * BT)
                for h in range(HALVES):
                    i = b * HALVES + h
                    cols = slice(h * BANK, (h + 1) * BANK)
                    for c in range(KE):
                        if c >= 2:
                            pe.wait_ge(S["gate"], i * KE + c - 1)
                        for k in range(KD):
                            o = W256["skip"][0] + c * P
                            last = nc.tensor.matmul(bank[c % 2][:, :], w256[:, k, o:o + P], xn[:, k, cols],
                                                    start=k == 0, stop=k == KD - 1)
                        last.then_inc(S["skip_done"], 1)
                    for c in range(KE):
                        if c >= 2:
                            pe.wait_ge(S["pre"], i * KE + c - 1)
                        for k in range(KD):
                            o = W256["in"][0] + c * P
                            last = nc.tensor.matmul(bank[2 + c % 2][:, :], w256[:, k, o:o + P], xn[:, k, cols],
                                                    start=k == 0, stop=k == KD - 1)
                        last.then_inc(S["in_done"], 1)
                    for c in range(KE):
                        pe.wait_ge(S["x"], i * KE + c + 1)
                        last = nc.tensor.matmul(bank[4][0:XROWS, :], col("xproj", c, XROWS), x[:, c, :],
                                                start=c == 0, stop=c == KE - 1)
                    last.then_inc(S["xproj"], 1)
                    pe.wait_ge(S["rank"], i + 1)
                    pe.wait_ge(S["gate"], (i + 1) * KE)
                    for c in range(KE):
                        nc.tensor.matmul(bank[c][:, :], w64[:, c * P:(c + 1) * P], rank[:, :], start=True, stop=True)\
                            .then_inc(S["dt_done"], 1)
                    pe.wait_ge(S["parts"], i + 1)
                    pe.wait_ge(S["v"], (i + 1) * KE)
                    for n in range(N + 1):
                        j = i * N + n
                        if n < N:
                            if n > 0:
                                pe.wait_ge(S["brow"], j)
                            nc.tensor.matmul(bank[6][:, :], select[:, n, :], parts[:, :], start=True, stop=True)\
                                .then_inc(S["b_done"], 1)
                            if n > 0:
                                pe.wait_ge(S["hc"], j)
                            nc.tensor.matmul(bank[7][:, :], select[:, STATE + n, :], parts[:, :],
                                             start=True, stop=True).then_inc(S["c_done"], 1)
                        if n > 0:
                            m = n - 1
                            pe.wait_ge(S["hc"], j)
                            for c in range(KE):
                                last = nc.tensor.matmul(bank[c][:, :], ident[:, :], hc[:, m % 2, c, :],
                                                        start=m == 0, stop=m == N - 1)
                            last.then_inc(S["y_part"], 1)
                    pe.wait_ge(S["y"], (i + 1) * KE)
                    for t in range(HT):
                        if t >= 2:
                            pe.wait_ge(S["added"], i * HT + t - 1)
                        for c in range(KE):
                            last = nc.tensor.matmul(bank[4 + t % 2][:, 0:DIM], y[:, 1, c, t * P:(t + 1) * P],
                                                    col("out", c, DIM), start=c == 0, stop=c == KE - 1)
                        last.then_inc(S["out"], 1)
                    pe.wait_ge(S["added"], (i + 1) * HT)


def build(nc, x_in, w256_in, w512_in, w128_in, w64_in, out):
    with ExitStack() as ctx:
        sb = lambda n, s, d=F32: ctx.enter_context(nc.sbuf_tensor(n, s, d))
        mem = {
            "x_tok": sb("x_tok", [P, TILES, DIM]),
            "w256": sb("w256", [P, KD, W256_COLS]),
            "w512": sb("w512", [P, KE, W512_COLS]),
            "w128": sb("w128", [P, W128_COLS]),
            "w64": sb("w64", [RANK, W64_COLS]),
            "ident": sb("ident", [P, P]),
            "select": sb("select", [96, 2 * STATE, P], BF16),
            "sign": sb("sign", [P, 1]),
            "eps": sb("eps", [P, 1]),
        }
        load_sem = {n: ctx.enter_context(nc.semaphore(f"load_{n}")) for n in ("x", "x0", "x1", "x2", "x3", "weights", "ident", "select")}
        ins = {
            "x": x_in.rearrange("b (t p) d -> p (b t) d", p=P),
            "w256": w256_in.rearrange("(k p) f -> p k f", p=P),
            "w512": w512_in.rearrange("(k p) f -> p k f", p=P),
            "w128": w128_in, "w64": w64_in,
        }
        setup(nc, mem, load_sem, ins)
        ffn(nc, None, mem, "f1", load_sem, None)
        mamba(nc, mem)
        ffn(nc, None, mem, "f2", None, out.rearrange("b (t p) d -> p (b t) d", p=P))


def kernel(**inputs):
    import numpy as np
    import concourse.bacc as bacc
    from concourse.bass_utils import run_bass_kernel_spmd

    a = {n: np.asarray(v) for n, v in inputs.items()}
    f = lambda n: a["L0_ffn_" + n]
    m = lambda n: a["L0_attn_" + n]
    col = lambda v: v.reshape(-1, 1)
    rows = lambda v, n: np.broadcast_to(v.reshape(1, -1), (n, v.size))
    arrays = {
        "x_in": m("resid"),
        "w256_in": np.concatenate([m("in_w").T, m("skip_w").T, f("cn_w1"), f("cn_w2"), f("gc_w1")], axis=1),
        "w512_in": np.concatenate([m("wd1").T, m("wB").T, m("wC").T, m("out_w").T, m("conv_w"), col(m("conv_b")),
                                   col(m("W_D")), col(m("wd2_b")), m("A_log")], axis=1),
        "w128_in": np.concatenate([
            f("cn_w3"), f("gc_w2"), np.broadcast_to(np.concatenate([f("cn_w4")] * 2, axis=0), (P, P)),
            col(f("cn_b2")), col(f("gc_b1")), m("norm_w").reshape(KD, P).T, f("cn_b1").reshape(KD, P).T,
            col(np.concatenate([f("cn_b3")] * 2)), rows(f("cn_b4"), P), rows(f("gc_b3"), P),
            rows(f("adaptive_range"), P)], axis=1),
        "w64_in": np.concatenate([m("wd2").T, np.broadcast_to(f("gc_w3"), (H3, P)), col(f("gc_b2"))], axis=1),
    }
    arrays = {n: np.ascontiguousarray(v) for n, v in arrays.items()}
    nc = bacc.Bacc("TRN2", target_bir_lowering=False, num_devices=1)
    args = [nc.dram_tensor(n, v.shape, mybir.dt.from_np(v.dtype), kind="ExternalInput").ap()
            for n, v in arrays.items()]
    out = nc.dram_tensor("out", arrays["x_in"].shape, F32, kind="ExternalOutput").ap()
    build(nc, *args, out)
    return run_bass_kernel_spmd(nc, [arrays], core_ids=[0]).results[0]["out"]
```

```python
from contextlib import ExitStack

import concourse.bass as bass
from concourse import mybir

F32 = mybir.dt.float32
BF16 = mybir.dt.bfloat16
ALU = mybir.AluOpType
ACT = mybir.ActivationFunctionType
AX = mybir.AxisListType

P = 128
BATCH, SEQ, DIM = 4, 1024, 256
INNER, STATE, RANK, TAPS = 512, 16, 64, 4
EPS = 1e-5
KD = DIM // P
KE = INNER // P
TILES = BATCH * SEQ // P
BT = SEQ // P
BANK = 512
HALVES = SEQ // BANK
XROWS = RANK + 2 * STATE
H3 = 64
CYCLES = 3

W256 = {"in": (0, INNER), "skip": (INNER, INNER), "w1": (2 * INNER, DIM), "w2": (2 * INNER + DIM, P),
        "g1": (2 * INNER + DIM + P, P)}
W256_COLS = 2 * INNER + DIM + 2 * P
W512 = {"xproj": (0, XROWS), "out": (XROWS, DIM), "conv": (XROWS + DIM, TAPS)}
_o = XROWS + DIM + TAPS
W512.update({"conv_b": (_o, 1), "D": (_o + 1, 1), "dt_b": (_o + 2, 1), "A_log": (_o + 3, STATE)})
W512_COLS = _o + 3 + STATE
W128 = {"w3": (0, H3), "g2": (H3, H3), "w4": (2 * H3, P)}
_o = 2 * H3 + P
for _n, _w in (("b2", 1), ("gb1", 1), ("norm", KD), ("b1", KD), ("b3", 1), ("b4", 1), ("gb3", 1), ("ar", 1)):
    W128[_n] = (_o, _w)
    _o += _w
W128_COLS = _o
W64 = {"dt": (0, INNER), "g3": (INNER, P), "gb2": (INNER + P, 1)}
W64_COLS = INNER + P + 1


class Chain:

    def __init__(self, engine, sem, per_turn=0, turn=0):
        self.engine, self.sem, self.count, self.per_turn, self.turn = engine, sem, 0, per_turn, turn

    def __call__(self, instruction):
        self.count += 1
        instruction.then_inc(self.sem, 1)
        self.engine.wait_ge(self.sem, self.turn * self.per_turn + self.count)

    def end(self):
        assert self.count == self.per_turn, self.count


def ffn(nc, sems, mem, name, load_sem, store):
    GROUP = 2
    TURNS = BATCH // GROUP
    GT = GROUP * BT
    STEPS = CYCLES * GROUP
    VEC_CHAIN = 1 + 1 + 3
    x_tok, w256, w128, w64 = mem["x_tok"], mem["w256"], mem["w128"], mem["w64"]
    ident, sign = mem["ident"], mem["sign"]
    with ExitStack() as ctx:
        sb = lambda n, s, d=F32: ctx.enter_context(nc.sbuf_tensor(f"{name}_{n}", s, d))
        sem = lambda n: ctx.enter_context(nc.semaphore(f"{name}_{n}"))
        bank = [ctx.enter_context(nc.psum_tensor(f"{name}_bank{i}", [P, BANK], F32)) for i in range(8)]
        stats = sb("stats", [P, GT, 6])
        scratch = sb("scratch", [P, 1])
        moments = sb("moments", [P, GT, 2])
        std = sb("std", [P, GT])
        rstd = sb("rstd", [P, GT])
        z_tok = sb("z_tok", [P, 4, DIM])
        state = sb("state", [P, KD, GROUP * SEQ])
        total = sb("total", [P, KD, GROUP])
        g1 = sb("g1", [P, GROUP])
        g2 = sb("g2", [H3, GROUP])
        gt = sb("gt", [P, GROUP])
        base = sb("base", [P, GROUP])
        slope = sb("slope", [P, 1])
        half_b4 = sb("half_b4", [P, 2])
        h1 = sb("h1", [P, KD, SEQ])
        h2 = sb("h2", [P, SEQ])
        h3 = sb("h3", [P, BANK])
        th = sb("th", [P, SEQ])
        couple = sb("couple", [P, SEQ])
        turned = sb("turned", [P, KD, SEQ])

        moments_ready, std_ready, z_ready = sem("moments"), sem("std"), sem("z")
        tr_ready, state_in, total_ready = sem("tr"), sem("state_in"), sem("total")
        pe_g, act_g, base_ready = sem("pe_g"), sem("act_g"), sem("base")
        l1_done, l2_done, l3_done, l4_done = sem("l1"), sem("l2"), sem("l3"), sem("l4")
        h1_ready, h2_ready, h3_ready, th_ready = sem("h1r"), sem("h2r"), sem("h3r"), sem("thr")
        updated, back_ready, back_added = sem("updated"), sem("back"), sem("added")
        vec, vec2, stored = sem("vec"), sem("vec2"), sem("stored")
        block = ctx.enter_context(nc.Block())

        def w(t, table, key, k=None):
            o, n = table[key]
            return t[:, k, o:o + n] if k is not None else t[:, o:o + n]

        @block.vector
        def _(dve):
            if load_sem is not None:
                dve.wait_ge(load_sem["weights"], 64)
            nc.vector.tensor_scalar(half_b4[:, 0:1], w(w128, W128, "b4"), 0.5, None, ALU.mult)
            nc.vector.tensor_scalar(half_b4[:, 1:2], w(w128, W128, "gb3"), 0.5, None, ALU.mult)
            nc.vector.tensor_scalar(slope[:, :], w(w128, W128, "ar"), sign[:, 0:1], 0.3, ALU.mult, ALU.mult)\
                .then_inc(vec2, 1)
            with dve.Fori(0, TURNS) as g:
                chain = Chain(dve, vec, VEC_CHAIN, g)
                for t in range(GT):
                    if load_sem is not None and t % BT == 0:
                        dve.wait_ge(load_sem["x"], g * GROUP + t // BT + 1)
                    last = nc.vector.bn_stats(stats[:, t, :], x_tok[:, g * GT + t, :])
                chain(last)
                nc.vector.memset(scratch[:, :], 0.0)
                for t in range(GT):
                    last = nc.vector.bn_aggr(moments[:, t, :], stats[:, t, :])
                last.then_inc(moments_ready, 1)
                dve.wait_ge(std_ready, g + 1)
                chain(nc.vector.reciprocal(rstd[:, :], std[:, :]))
                for t in range(GT):
                    if t >= 4:
                        dve.wait_ge(tr_ready, g * GT + t - 3)
                    nc.vector.tensor_scalar(z_tok[:, t % 4, :], x_tok[:, g * GT + t, :], moments[:, t, 0:1],
                                            rstd[:, t:t + 1], ALU.subtract, ALU.mult).then_inc(z_ready, 1)
                dve.wait_ge(state_in, (g + 1) * GT // 2)
                nc.vector.tensor_reduce(total[:, :, :], state[:, :, :].rearrange("p k (b n) -> p k b n", b=GROUP),
                                        AX.X, ALU.add).then_inc(total_ready, 1)
                dve.wait_ge(act_g, (g + 1) * 3)
                chain(nc.vector.tensor_scalar(base[:, :], gt[:, :], w(w128, W128, "ar"), 0.7, ALU.mult, ALU.mult))
                chain(nc.vector.tensor_scalar(gt[:, :], base[:, :], 0.1, None, ALU.add))
                chain(nc.vector.tensor_scalar(base[:, :], gt[:, :], sign[:, 0:1], None, ALU.mult))
                chain.end()
                steps = Chain(dve, updated, STEPS * HALVES * 5, g)
                for s in range(STEPS):
                    b = s % GROUP
                    for h in range(HALVES):
                        c = slice(h * BANK, (h + 1) * BANK)
                        cs = slice(b * SEQ + h * BANK, b * SEQ + (h + 1) * BANK)
                        dve.wait_ge(th_ready, (g * STEPS + s) * HALVES + h + 1)
                        steps(nc.vector.tensor_scalar(couple[:, c], th[:, c], slope[:, 0:1], base[:, b:b + 1],
                                                      ALU.mult, ALU.add))
                        nc.vector.tensor_tensor(turned[:, 0, c], couple[:, c], state[:, 1, cs], ALU.mult)\
                            .then_inc(updated, 1)
                        nc.vector.tensor_tensor(turned[:, 1, c], couple[:, c], state[:, 0, cs], ALU.mult)\
                            .then_inc(updated, 1)
                        steps.count += 2
                        dve.wait_ge(updated, g * steps.per_turn + steps.count)
                        nc.vector.tensor_tensor(state[:, 0, cs], state[:, 0, cs], turned[:, 0, c], ALU.add)\
                            .then_inc(updated, 1)
                        nc.vector.tensor_tensor(state[:, 1, cs], state[:, 1, cs], turned[:, 1, c], ALU.subtract)\
                            .then_inc(updated, 1)
                        steps.count += 2
                steps.end()
                for t in range(GT // 2):
                    dve.wait_ge(back_ready, g * (GT // 2) + t + 1)
                    nc.vector.scalar_tensor_tensor(
                        x_tok[:, bass.ds(g * GT + 2 * t, 2), :],
                        bank[t % 4][:, :].rearrange("p (a d) -> p a d", a=2), 0.5,
                        x_tok[:, bass.ds(g * GT + 2 * t, 2), :], ALU.mult, ALU.add).then_inc(back_added, 1)

        @block.tensor
        def _(pe):
            if load_sem is not None:
                pe.wait_ge(load_sem["weights"], 64)
                pe.wait_ge(load_sem["ident"], 2)
            with pe.Fori(0, TURNS) as g:
                for t in range(GT):
                    if t % 2 == 0 and t >= 8:
                        pe.wait_ge(state_in, g * (GT // 2) + t // 2 - 3)
                    pe.wait_ge(z_ready, g * GT + t + 1)
                    for k in range(KD):
                        o = (2 * k + t % 2) * P
                        last = nc.tensor.transpose(bank[t // 2 % 4][:, o:o + P], z_tok[:, t % 4, k * P:(k + 1) * P],
                                                   ident[:, :])
                    last.then_inc(tr_ready, 1)
                pe.wait_ge(total_ready, g + 1)
                for k in range(KD):
                    last = nc.tensor.matmul(bank[7][:, 0:GROUP], w(w256, W256, "g1", k), total[:, k, :],
                                            start=k == 0, stop=k == KD - 1)
                last.then_inc(pe_g, 1)
                pe.wait_ge(act_g, g * 3 + 1)
                nc.tensor.matmul(bank[6][0:H3, 0:GROUP], w(w128, W128, "g2"), g1[:, :], start=True, stop=True)\
                    .then_inc(pe_g, 1)
                pe.wait_ge(act_g, g * 3 + 2)
                nc.tensor.matmul(bank[5][:, 0:GROUP], w(w64, W64, "g3"), g2[:, :], start=True, stop=True)\
                    .then_inc(pe_g, 1)

                def layer1(s, h, m):
                    b = s % GROUP
                    if s > 0:
                        pe.wait_ge(h1_ready, (g * STEPS + s - 1) * 4 + h * 2 + m + 1)
                    else:
                        pe.wait_ge(state_in, (g + 1) * (GT // 2))
                    if s >= GROUP:
                        pe.wait_ge(updated, g * STEPS * HALVES * 5 + ((s - GROUP) * HALVES + h + 1) * 5)
                    for k in range(KD):
                        o = W256["w1"][0] + m * P
                        last = nc.tensor.matmul(bank[h * 2 + m][:, :], w256[:, k, o:o + P],
                                                state[:, k, b * SEQ + h * BANK:b * SEQ + (h + 1) * BANK],
                                                start=k == 0, stop=k == KD - 1)
                    last.then_inc(l1_done, 1)

                def layer2(s, h):
                    pe.wait_ge(h1_ready, (g * STEPS + s) * 4 + h * 2 + 2)
                    if s > 0 and h == 0:
                        pe.wait_ge(th_ready, (g * STEPS + s) * HALVES)
                    if s > 0 and h == 1:
                        pe.wait_ge(h2_ready, (g * STEPS + s) * HALVES)
                    for k in range(KD):
                        last = nc.tensor.matmul(bank[4 + h][:, :], w(w256, W256, "w2", k),
                                                h1[:, k, h * BANK:(h + 1) * BANK], start=k == 0, stop=k == KD - 1)
                    last.then_inc(l2_done, 1)

                def layer3(s):
                    pe.wait_ge(h2_ready, (g * STEPS + s) * HALVES + 2)
                    for h in range(HALVES):
                        last = nc.tensor.matmul(bank[6][h * H3:(h + 1) * H3, :], w(w128, W128, "w3"),
                                                h2[:, h * BANK:(h + 1) * BANK], start=True, stop=True)
                    last.then_inc(l3_done, 1)

                def layer4(s):
                    pe.wait_ge(h3_ready, g * STEPS + s + 1)
                    for h in range(HALVES):
                        o = W128["w4"][0]
                        last = nc.tensor.matmul(bank[7 if h == 0 else 4][:, :],
                                                w128[h * H3:(h + 1) * H3, o:o + P],
                                                h3[h * H3:(h + 1) * H3, :], start=True, stop=True)
                    last.then_inc(l4_done, 1)

                pe.wait_ge(act_g, g * 3 + 3)
                for s in range(STEPS + 1):
                    if s < STEPS:
                        layer1(s, 0, 0)
                    if s > 0:
                        layer3(s - 1)
                    if s < STEPS:
                        layer1(s, 0, 1)
                    if s > 0:
                        layer4(s - 1)
                    if s < STEPS:
                        layer1(s, 1, 0)
                        layer1(s, 1, 1)
                        layer2(s, 0)
                        layer2(s, 1)
                for t in range(GT):
                    if t % 2 == 0:
                        if t >= 8:
                            pe.wait_ge(back_added, g * (GT // 2) + t // 2 - 3)
                        b, h = t // BT, t % BT * P // BANK
                        pe.wait_ge(updated, g * STEPS * HALVES * 5 + ((STEPS - GROUP + b) * HALVES + h + 1) * 5)
                    for k in range(KD):
                        o = (t % 2) * DIM + k * P
                        last = nc.tensor.transpose(bank[t // 2 % 4][:, o:o + P], state[:, k, t * P:(t + 1) * P],
                                                   ident[:, :])
                    if t % 2:
                        last.then_inc(back_ready, 1)
                pe.wait_ge(back_added, (g + 1) * (GT // 2))

        @block.scalar
        def _(act):
            if load_sem is not None:
                act.wait_ge(load_sem["weights"], 64)
            act.wait_ge(vec2, 1)
            with act.Fori(0, TURNS) as g:
                act.wait_ge(moments_ready, g + 1)
                nc.scalar.activation(std[:, :], moments[:, :, 1], ACT.Sqrt, bias=mem["eps"][:, 0:1])\
                    .then_inc(std_ready, 1)
                for t in range(GT // 2):
                    act.wait_ge(tr_ready, g * GT + 2 * t + 2)
                    nc.scalar.activation(state[:, :, 2 * t * P:2 * (t + 1) * P],
                                         bank[t % 4][:, :].rearrange("p (k n) -> p k n", k=KD),
                                         ACT.Copy).then_inc(state_in, 1)
                act.wait_ge(pe_g, g * 3 + 1)
                nc.scalar.activation(g1[:, :], bank[7][:, 0:GROUP], ACT.Gelu, bias=w(w128, W128, "gb1"),
                                     scale=1.0 / SEQ).then_inc(act_g, 1)
                act.wait_ge(pe_g, g * 3 + 2)
                nc.scalar.activation(g2[:, :], bank[6][0:H3, 0:GROUP], ACT.Gelu, bias=w64[:, W64["gb2"][0]:][:, 0:1])\
                    .then_inc(act_g, 1)
                act.wait_ge(pe_g, g * 3 + 3)
                nc.scalar.activation(gt[:, :], bank[5][:, 0:GROUP], ACT.Tanh, bias=half_b4[:, 1:2], scale=0.5)\
                    .then_inc(act_g, 1)

                def gelu1(s, h, m):
                    act.wait_ge(l1_done, (g * STEPS + s) * 4 + h * 2 + m + 1)
                    o = W128["b1"][0] + m
                    nc.scalar.activation(h1[:, m, h * BANK:(h + 1) * BANK], bank[h * 2 + m][:, :], ACT.Gelu,
                                         bias=w128[:, o:o + 1]).then_inc(h1_ready, 1)

                def gelu2(s, h):
                    act.wait_ge(l2_done, (g * STEPS + s) * HALVES + h + 1)
                    nc.scalar.activation(h2[:, h * BANK:(h + 1) * BANK], bank[4 + h][:, :], ACT.Gelu,
                                         bias=w(w128, W128, "b2")).then_inc(h2_ready, 1)

                def gelu3(s):
                    act.wait_ge(l3_done, g * STEPS + s + 1)
                    nc.scalar.activation(h3[:, :], bank[6][:, :], ACT.Gelu, bias=w(w128, W128, "b3"))\
                        .then_inc(h3_ready, 1)

                def tanh4(s, h):
                    act.wait_ge(l4_done, g * STEPS + s + 1)
                    if s > 0:
                        act.wait_ge(updated, g * STEPS * HALVES * 5 + ((s - 1) * HALVES + h + 1) * 5)
                    nc.scalar.activation(th[:, h * BANK:(h + 1) * BANK], bank[7 if h == 0 else 4][:, :], ACT.Tanh,
                                         bias=half_b4[:, 0:1], scale=0.5).then_inc(th_ready, 1)

                for s in range(STEPS + 1):
                    if s < STEPS:
                        gelu1(s, 0, 0)
                    if s > 0:
                        gelu3(s - 1)
                    if s < STEPS:
                        gelu1(s, 0, 1)
                    if s > 0:
                        tanh4(s - 1, 0)
                        tanh4(s - 1, 1)
                    if s < STEPS:
                        gelu1(s, 1, 0)
                        gelu1(s, 1, 1)
                        gelu2(s, 0)
                        gelu2(s, 1)

        if load_sem is not None:
            @block.sync
            def _(sp):
                for b in range(BATCH):
                    sp.wait_ge(load_sem[f"x{b}"], 16)
                    sp.sem_inc(load_sem["x"], 1)

        if store is not None:
            @block.sync
            def _(sp):
                with sp.Fori(0, TURNS) as g:
                    sp.wait_ge(back_added, (g + 1) * (GT // 2))
                    sp.dma_start(store[:, bass.ds(g * GT, GT), :], x_tok[:, bass.ds(g * GT, GT), :])\
                        .then_inc(stored, 16)
                sp.wait_ge(stored, TURNS * 16)


def setup(nc, mem, load_sem, ins):
    x_tok = mem["x_tok"]
    with nc.Block() as block:
        @block.sync
        def _(sp):
            for b in range(BATCH):
                sp.dma_start(x_tok[:, b * BT:(b + 1) * BT, :], ins["x"][:, b * BT:(b + 1) * BT, :])\
                    .then_inc(load_sem[f"x{b}"], 16)

        @block.scalar
        def _(act):
            for n in ("w256", "w128", "w64", "w512"):
                act.dma_start(mem[n][...], ins[n]).then_inc(load_sem["weights"], 16)

        @block.vector
        def _(dve):
            nc.vector.memset(mem["eps"][:, :], EPS)
            nc.vector.memset(mem["sign"][0:H3, :], 1.0)
            nc.vector.memset(mem["sign"][H3:P, :], -1.0)

        @block.gpsimd
        def _(pool):
            nc.gpsimd.memset(mem["ident"][:, :], 0.0).then_inc(load_sem["ident"], 1)
            nc.gpsimd.memset(mem["select"][:, :, :], 0.0).then_inc(load_sem["select"], 1)
            pool.wait_ge(load_sem["ident"], 1)
            nc.gpsimd.affine_select(out=mem["ident"][:, :], in_=mem["ident"][:, :], compare_op=ALU.not_equal,
                                    fill=1.0, base=0, pattern=[[-1, P]], channel_multiplier=1)\
                .then_inc(load_sem["ident"], 1)
            for a in range(3):
                pool.wait_ge(load_sem["select"], a + 1)
                nc.gpsimd.affine_select(out=mem["select"][:, :, :], in_=mem["select"][:, :, :],
                                        compare_op=ALU.not_equal, fill=1.0, base=-32 * a,
                                        pattern=[[-1, STATE], [0, P]], channel_multiplier=1)\
                    .then_inc(load_sem["select"], 1)


def mamba(nc, mem, b_rows):
    x_tok, w256, w512, w64, w128 = mem["x_tok"], mem["w256"], mem["w512"], mem["w64"], mem["w128"]
    ident, select, eps = mem["ident"], mem["select"], mem["eps"]
    HT = BANK // P
    SEGS = BATCH * HALVES
    N = STATE
    PLAN = [(0, 1, "turn", 0), (0, 2, "turn", 1), (1, 1, "in", 0), (1, 2, "in", 1), (2, 1, "in", 2), (2, 2, "in", 3),
            (3, 1, "out", 0), (4, 1, "out", 1), (5, 1, "xproj", 0), (5, 2, "skip", 0), (6, 1, "dt", 0),
            (6, 2, "dt", 1), (7, 1, "dt", 2), (7, 2, "dt", 3), (8, 1, "skip", 1), (9, 1, "skip", 2),
            (10, 1, "skip", 3)]

    class Segment:

        def __init__(self, i, parity, core=True, prep=True, out=True, base=None, first=False):
            self.i, self.h, self.core, self.prep, self.out, self.first = i, parity, core, prep, out, first
            self.p = i + 1
            self.ph = 1 - parity
            kinds = {"turn": prep, "in": prep, "xproj": prep, "dt": prep, "skip": core, "out": out}
            self.plan = [w for w in PLAN if kinds[w[2]]]
            self.base = base

        def place(self, kind, c):
            return self.base + [w[2:] for w in self.plan].index((kind, c))

        def at(self, n, slot):
            return [w[2:] for w in self.plan if w[0] == n and w[1] == slot]

    FULL = len(PLAN)
    prologue = Segment(-1, 1, core=False, out=False, base=0)
    head = Segment(0, 0, out=False, base=len(prologue.plan), first=True)
    after_head = head.base + len(head.plan)
    last = Segment(SEGS - 1, 1, prep=False, base=after_head + FULL * (SEGS - 2))
    tail = Segment(SEGS, 0, core=False, prep=False, base=last.base + len(last.plan))

    def middle(k):
        return [Segment(2 * k + 1 + d, 1 - d, base=after_head + FULL * (2 * k + d)) for d in range(2)]

    def run(engine, segment):
        segment(prologue)
        segment(head)
        with engine.Fori(0, (SEGS - 2) // 2) as k:
            for s in middle(k):
                segment(s)
        segment(last)
        segment(tail)

    with ExitStack() as ctx:
        sb = lambda n, s, d=F32: ctx.enter_context(nc.sbuf_tensor(f"m_{n}", s, d))
        sem = lambda n: ctx.enter_context(nc.semaphore(f"m_{n}"))
        bank = [ctx.enter_context(nc.psum_tensor(f"m_bank{i}", [P, BANK], F32)) for i in range(8)]
        scratch = sb("scratch", [P, 1])
        stats = sb("stats", [P, TILES, 6])
        moments = sb("moments", [P, TILES, 2])
        root = sb("root", [P, TILES])
        square = sb("square", [P, TILES])
        rstd = sb("rstd", [P, TILES])
        rrms = sb("rrms", [P, TILES])
        xn = sb("xn", [P, 2, KD, BANK])
        negA = sb("negA", [P, KE, STATE])
        expA = sb("expA", [P, KE, STATE])
        conv = sb("conv", [P, KE, TAPS + 1])
        pre = sb("pre", [P, KE, TAPS - 1 + BANK])
        th = sb("th", [P, 2, BANK])
        gate = sb("gate", [P, KE, BANK])
        x = sb("x", [P, 2, KE, BANK])
        proj = sb("proj", [XROWS, BANK])
        parts = sb("parts", [RANK + STATE, 2, BANK], BF16)
        tmp_u = sb("tmp_u", [P, KE, BANK])
        delta = sb("delta", [P, 2, KE, BANK])
        dx = sb("dx", [P, 2, KE, BANK])
        brow = sb("brow", [P, 2, 2, BANK])
        u = sb("u", [P, 2, KE, BANK])
        hid = sb("hid", [P, 2, KE, BANK])
        carry = sb("carry", [P, STATE, KE])
        hc = sb("hc", [P, 2, KE, BANK])
        xn_tok = tmp_u[:, 0:2, :].rearrange("p a (b d) -> p (a b) d", d=DIM)
        z_tok = tmp_u[:, 2:4, :].rearrange("p a (b d) -> p (a b) d", d=DIM)
        acc, th_x = [dx[:, a, 0:2] for a in range(2)], [dx[:, a, 2:4] for a in range(2)]
        rest = [dx[0:RANK + STATE, a, 0] for a in range(2)]
        mid = [dx[0:RANK + STATE, a, 1].bitcast(BF16)[:, 0:BANK] for a in range(2)]

        S = {n: sem(n) for n in (
            "negA", "conv_w", "stats", "moments", "root", "square", "rstd", "z", "xn_tok", "z_added", "work_done",
            "work_free", "history", "taps", "conv", "tanh_x", "x", "gate", "parts", "split", "abs", "e", "u1", "corr",
            "ln", "log1p", "delta", "dx", "b_stored", "b_there", "brow0", "brow1", "u", "a", "scan", "carry", "c_done", "hc",
            "y_part", "yd", "y", "out_added", "expA", "zeroed")}
        block = ctx.enter_context(nc.Block())

        def col(key, c, n=1):
            o = W512[key][0]
            return w512[:, c, o:o + n]

        @block.sync
        def _(sp):
            def segment(s):
                def load(i, h, q, fresh=False):
                    if not fresh:
                        sp.wait_ge(S["u"], i * N + 2 * q - 2)
                    sp.dma_start(brow[:, q % 2, :, :],
                                 b_rows[h, 2 * q:2 * q + 2, :].unsqueeze(0).to_broadcast([P, 2, BANK]))\
                        .then_inc(S[f"brow{q % 2}"], 16)

                if s.core:
                    for q in range(2, 7):
                        load(s.i, s.h, q)
                if s.prep:
                    sp.wait_ge(S["work_free"], s.place("xproj", 0) + 1)
                    sp.dma_start(b_rows[s.ph], proj[RANK + STATE:XROWS, :]).then_inc(S["b_stored"], 16)
                if s.core:
                    load(s.i, s.h, 7)
                if s.prep:
                    sp.wait_ge(S["b_stored"], 16 * (s.p + 1))
                    sp.sem_inc(S["b_there"], 1)
                    load(s.p, s.ph, 0, fresh=not s.core)
                    load(s.p, s.ph, 1, fresh=not s.core)

            run(sp, segment)

        @block.scalar
        def _(act):
            o = W512["A_log"][0]
            nc.scalar.activation(expA[:, :, :], w512[:, :, o:o + STATE], ACT.Exp).then_inc(S["expA"], 1)
            act.wait_ge(S["expA"], 1)
            nc.scalar.mul(negA[:, :, :], expA[:, :, :], -1.0).then_inc(S["negA"], 1)
            act.wait_ge(S["moments"], 1)
            nc.scalar.activation(root[:, :], moments[:, :, 1], ACT.Sqrt, bias=eps[:, 0:1]).then_inc(S["root"], 1)
            act.wait_ge(S["square"], 2)
            nc.scalar.activation(root[:, :], square[:, :], ACT.Sqrt, bias=eps[:, 0:1]).then_inc(S["root"], 1)
            act.wait_ge(S["negA"], 1)

            def segment(s):
                i, p = s.i, s.p

                def decay(n, c):
                    j = i * N + n
                    if not (s.first and n == 0 and c < 2):
                        act.wait_ge(S["scan"], j * KE + c - 1)
                    nc.scalar.activation(bank[4 + c % 2][:, :], delta[:, s.h, c, :], ACT.Exp,
                                         scale=negA[:, c, n:n + 1]).then_inc(S["a"], 1)

                def evacuate(kind, c):
                    act.wait_ge(S["work_done"], s.place(kind, c) + 1)
                    b = bank[6]
                    if kind == "turn":
                        for k in range(KD):
                            o = W128["norm"][0] + k
                            op = nc.scalar.activation(xn[:, s.ph, k, c * 2 * P:(c + 1) * 2 * P],
                                                      b[:, k * 2 * P:(k + 1) * 2 * P], ACT.Copy,
                                                      scale=w128[:, o:o + 1])
                    elif kind == "in":
                        act.wait_ge(S["history"], p + 1)
                        op = nc.scalar.activation(pre[:, c, TAPS - 1:TAPS - 1 + BANK], b[:, :], ACT.Copy)
                    elif kind == "skip":
                        if c == 0 and not s.first:
                            act.wait_ge(S["out_added"], 2 * i)
                        if c >= 2:
                            act.wait_ge(S["gate"], i * KE + c - 1)
                        nc.scalar.activation(th[:, c % 2, :], b[:, :], ACT.Tanh, scale=0.5)
                        op = nc.scalar.activation(gate[:, c, :], b[:, :], ACT.Copy)
                    elif kind == "xproj":
                        if s.core:
                            act.wait_ge(S["b_stored"], 16 * p)
                            act.wait_ge(S["parts"], p)
                        op = nc.scalar.activation(proj[:, :], b[0:XROWS, :], ACT.Copy)
                    elif kind == "dt":
                        op = nc.scalar.activation(delta[:, s.ph, c, :], b[:, :], ACT.Identity, bias=col("dt_b", c))
                    elif kind == "out":
                        act.wait_ge(S["gate"], i * KE)
                        op = nc.scalar.activation(th[:, c, :], b[:, :], ACT.Copy)
                    op.then_inc(S["work_free"], 1)

                for n in range(N + 1):
                    if s.core and n < N:
                        if n == 0:
                            act.wait_ge(S["delta"], 2 * (i + 1))
                        decay(n, 0)
                        decay(n, 1)
                    for w in s.at(n - 2, 2):
                        evacuate(*w)
                    if s.core and n < N:
                        decay(n, 2)
                        decay(n, 3)
                    for w in s.at(n - 1, 1):
                        evacuate(*w)
                    if not s.prep:
                        continue
                    if n in (4, 5):
                        for c in (2 * (n - 4), 2 * (n - 4) + 1):
                            act.wait_ge(S["conv"], p * KE + c + 1)
                            nc.scalar.activation(th_x[s.ph][:, c % 2], acc[s.ph][:, c % 2], ACT.Tanh).then_inc(S["tanh_x"], 1)
                    if n in (9, 10):
                        g = n - 9
                        cs = slice(2 * g, 2 * g + 2)
                        act.wait_ge(S["work_free"], s.place("dt", 2 * g + 1) + 1)
                        act.wait_ge(S["x"], (p + 1) * KE)
                        act.wait_ge(S["parts"], p + 1)
                        nc.scalar.activation(dx[:, s.ph, cs], delta[:, s.ph, cs], ACT.Abs).then_inc(S["abs"], 1)
                        act.wait_ge(S["abs"], 2 * p + g + 1)
                        nc.scalar.activation(dx[:, s.ph, cs], dx[:, s.ph, cs], ACT.Exp, scale=-1.0)\
                            .then_inc(S["e"], 1)
                    if n == 12:
                        for g in range(2):
                            cs = slice(2 * g, 2 * g + 2)
                            act.wait_ge(S["corr"], 2 * p + g + 1)
                            nc.scalar.activation(tmp_u[:, cs], tmp_u[:, cs], ACT.Ln).then_inc(S["ln"], 1)

            run(act, segment)

        @block.gpsimd
        def _(pool):
            def segment(s):
                i, p = s.i, s.p
                for n in range(N + 1):
                    if s.core and n < N:
                        j = i * N + n
                        if n == 0:
                            pool.wait_ge(S["dx"], 2 * (i + 1))
                        if n % 2 == 0:
                            pool.wait_ge(S[f"brow{n // 2 % 2}"], 16 * (i * 4 + n // 4 + 1))
                        if not (s.first and n < 2):
                            pool.wait_ge(S["scan"], (j - 1) * KE)
                        nc.gpsimd.tensor_tensor(
                            u[:, n % 2, :, :], dx[:, s.h, :, :],
                            brow[:, n // 2 % 2, n % 2, :].unsqueeze(1).to_broadcast([P, KE, BANK]),
                            ALU.mult).then_inc(S["u"], 1)
                    if s.prep and n == 3:
                        pool.wait_ge(S["z"], p + 1)
                        tiles = x_tok[:, bass.ds(p * HT, HT), :] if not isinstance(p, int) \
                            else x_tok[:, p * HT:(p + 1) * HT, :]
                        nc.gpsimd.tensor_tensor(tiles, tiles, z_tok, ALU.add).then_inc(S["z_added"], 1)
                    if s.out and n in (5, 6):
                        g = n - 5
                        pool.wait_ge(S["work_free"], s.place("out", g) + 1)
                        pool.wait_ge(S["z_added"], i)
                        at = (i - 1) * HT + 2 * g
                        tiles = x_tok[:, bass.ds(at, 2), :] if not isinstance(at, int) else x_tok[:, at:at + 2, :]
                        nc.gpsimd.tensor_tensor(tiles, tiles, th[:, g, :].rearrange("p (a d) -> p a d", d=DIM),
                                                ALU.add).then_inc(S["out_added"], 1)
                    if s.prep and n == 14:
                        for g in range(2):
                            cs = slice(2 * g, 2 * g + 2)
                            pool.wait_ge(S["ln"], 2 * p + g + 1)
                            nc.gpsimd.tensor_tensor(dx[:, s.ph, cs], tmp_u[:, cs], dx[:, s.ph, cs],
                                                    ALU.subtract).then_inc(S["log1p"], 1)
                    if s.prep and n == 16:
                        for g in range(2):
                            cs = slice(2 * g, 2 * g + 2)
                            pool.wait_ge(S["delta"], 2 * p + g + 1)
                            nc.gpsimd.tensor_tensor(dx[:, s.ph, cs], delta[:, s.ph, cs], x[:, s.ph, cs],
                                                    ALU.mult).then_inc(S["dx"], 1)

            run(pool, segment)

        @block.vector
        def _(dve):
            o = W512["conv"][0]
            nc.vector.tensor_scalar(conv[:, :, :], w512[:, :, o:o + TAPS + 1], 0.5, None, ALU.mult)
            nc.vector.memset(pre[:, :, 0:TAPS - 1], 0.0).then_inc(S["history"], 1)
            nc.vector.memset(parts[:, :, :], 0.0).then_inc(S["zeroed"], 1)
            for t in range(TILES):
                op = nc.vector.bn_stats(stats[:, t, :], x_tok[:, t, :])
            op.then_inc(S["stats"], 1)
            dve.wait_ge(S["zeroed"], 1)
            dve.wait_ge(S["stats"], 1)
            for t in range(TILES):
                op = nc.vector.bn_aggr(moments[:, t, :], stats[:, t, :])
            op.then_inc(S["moments"], 1)
            dve.wait_ge(S["root"], 1)
            nc.vector.reciprocal(rstd[:, :], root[:, :]).then_inc(S["rstd"], 1)
            dve.wait_ge(S["rstd"], 1)
            nc.vector.tensor_tensor(square[:, :], rstd[:, :], rstd[:, :], ALU.mult).then_inc(S["square"], 1)
            dve.wait_ge(S["square"], 1)
            nc.vector.tensor_tensor(square[:, :], square[:, :], moments[:, :, 1], ALU.mult).then_inc(S["square"], 1)
            dve.wait_ge(S["root"], 2)
            nc.vector.reciprocal(rrms[:, :], root[:, :]).then_inc(S["rstd"], 1)
            dve.wait_ge(S["rstd"], 2)

            def segment(s):
                i, p = s.i, s.p

                def scan(n, c):
                    j = i * N + n
                    dve.wait_ge(S["a"], j * KE + c + 1)
                    nc.vector.tensor_tensor_scan(
                        hid[:, n % 2, c, :], bank[4 + c % 2][:, :], u[:, n % 2, c, :],
                        0.0 if s.h == 0 else carry[:, n, c:c + 1], ALU.mult, ALU.add).then_inc(S["scan"], 1)

                def weigh(n, pair):
                    j = i * N + n
                    cs = slice(2 * pair, 2 * pair + 2)
                    if pair == 0:
                        dve.wait_ge(S["scan"], (j + 1) * KE)
                        if s.h == 0:
                            nc.vector.tensor_copy(carry[:, n, :], hid[:, n % 2, :, BANK - 1])\
                                .then_inc(S["carry"], 1)
                        dve.wait_ge(S["c_done"], j + 1)
                        if not (s.first and n < 2):
                            dve.wait_ge(S["y_part"], j - 1)
                    nc.vector.tensor_tensor(hc[:, n % 2, cs, :], hid[:, n % 2, cs, :],
                                            bank[7][:, :].unsqueeze(1).to_broadcast([P, 2, BANK]),
                                            ALU.mult).then_inc(S["hc"], 1)

                def finish():
                    dve.wait_ge(S["y_part"], i * N)
                    dve.wait_ge(S["gate"], i * KE)
                    for c in range(KE):
                        xc = x[:, 1 - s.h, c, :]
                        nc.vector.scalar_tensor_tensor(xc, xc, col("D", c), bank[c][:, :],
                                                       ALU.mult, ALU.add).then_inc(S["yd"], 1)
                    for c in range(KE):
                        dve.wait_ge(S["yd"], (i - 1) * KE + c + 1)
                        nc.vector.scalar_tensor_tensor(gate[:, c, :], x[:, 1 - s.h, c, :], 0.5, gate[:, c, :],
                                                       ALU.mult, ALU.mult).then_inc(S["y"], 1)

                def normalise():
                    if s.core:
                        dve.wait_ge(S["log1p"], 2 * p)
                    for t in range(HT):
                        at = p * HT + t
                        op = nc.vector.tensor_scalar(z_tok[:, t, :], x_tok[:, at, :], moments[:, at, 0:1],
                                                     rstd[:, bass.ds(at, 1)], ALU.subtract, ALU.mult)
                    op.then_inc(S["z"], 1)
                    dve.wait_ge(S["z"], p + 1)
                    for t in range(HT):
                        at = p * HT + t
                        op = nc.vector.tensor_scalar(xn_tok[:, t, :], z_tok[:, t, :], rrms[:, bass.ds(at, 1)], None,
                                                     ALU.mult)
                    op.then_inc(S["xn_tok"], 1)

                def convolve(c):
                    dve.wait_ge(S["work_free"], s.place("in", c) + 1)
                    if c >= 2:
                        dve.wait_ge(S["x"], p * KE + c - 1)
                    for k in range(TAPS):
                        a = acc[s.ph][:, c % 2]
                        if k == 0:
                            op = nc.vector.tensor_scalar(a, pre[:, c, 0:BANK], conv[:, c, 0:1],
                                                         conv[:, c, TAPS:TAPS + 1], ALU.mult, ALU.add)
                        else:
                            dve.wait_ge(S["taps"], (p * KE + c) * (TAPS - 1) + k)
                            op = nc.vector.scalar_tensor_tensor(a, pre[:, c, k:k + BANK], conv[:, c, k:k + 1], a,
                                                                ALU.mult, ALU.add)
                        op.then_inc(S["taps" if k < TAPS - 1 else "conv"], 1)

                def silu(c):
                    dve.wait_ge(S["tanh_x"], p * KE + c + 1)
                    nc.vector.scalar_tensor_tensor(x[:, s.ph, c, :], th_x[s.ph][:, c % 2], 1.0, acc[s.ph][:, c % 2],
                                                   ALU.add, ALU.mult).then_inc(S["x"], 1)

                def gate_skip(c):
                    dve.wait_ge(S["work_free"], s.place("skip", c) + 1)
                    nc.vector.scalar_tensor_tensor(gate[:, c, :], th[:, c % 2, :], 1.0, gate[:, c, :],
                                                   ALU.add, ALU.mult).then_inc(S["gate"], 1)

                def split_c():
                    R = slice(RANK, RANK + STATE)
                    dve.wait_ge(S["work_free"], s.place("xproj", 0) + 1)
                    links = p * 4
                    nc.vector.tensor_copy(parts[R, s.ph, :], proj[R, :]).then_inc(S["split"], 1)
                    dve.wait_ge(S["split"], links + 1)
                    nc.vector.tensor_tensor(rest[s.ph][R, :], proj[R, :], parts[R, s.ph, :], ALU.subtract)\
                        .then_inc(S["split"], 1)
                    dve.wait_ge(S["split"], links + 2)
                    nc.vector.tensor_copy(mid[s.ph][R, :], rest[s.ph][R, :]).then_inc(S["split"], 1)
                    dve.wait_ge(S["split"], links + 3)
                    nc.vector.tensor_copy(parts[0:STATE, s.ph, :], mid[s.ph][R, :]).then_inc(S["split"], 1)
                    nc.vector.tensor_tensor(parts[32:32 + STATE, s.ph, :], rest[s.ph][R, :], mid[s.ph][R, :], ALU.subtract)\
                        .then_inc(S["parts"], 1)

                def round_off(g):
                    cs = slice(2 * g, 2 * g + 2)
                    dve.wait_ge(S["e"], 2 * p + g + 1)
                    if g == 1:
                        dve.wait_ge(S["z_added"], p + 1)
                    nc.vector.tensor_scalar(tmp_u[:, cs], dx[:, s.ph, cs], 1.0, None, ALU.add).then_inc(S["u1"], 1)
                    dve.wait_ge(S["u1"], 2 * p + g + 1)
                    nc.vector.scalar_tensor_tensor(dx[:, s.ph, cs], tmp_u[:, cs], -1.0, dx[:, s.ph, cs],
                                                   ALU.add, ALU.subtract).then_inc(S["corr"], 1)

                def softplus(g):
                    cs = slice(2 * g, 2 * g + 2)
                    dve.wait_ge(S["log1p"], 2 * p + g + 1)
                    nc.vector.scalar_tensor_tensor(delta[:, s.ph, cs], delta[:, s.ph, cs], 0.0, dx[:, s.ph, cs],
                                                   ALU.max, ALU.add).then_inc(S["delta"], 1)

                for n in range(N + 1):
                    if s.core and n < N:
                        j = i * N + n
                        dve.wait_ge(S["u"], j + 1)
                        if n == 0 and s.h == 1:
                            dve.wait_ge(S["carry"], (i + 1) * N // 2 if isinstance(i, int) else (i + 1) * (N // 2))
                        if not (s.first and n < 2):
                            dve.wait_ge(S["hc"], 2 * (j - 1))
                    for pair in range(2):
                        if s.core and n < N:
                            scan(n, 2 * pair)
                            scan(n, 2 * pair + 1)
                        if s.core and n > 0:
                            weigh(n - 1, pair)
                    if n == 0 and s.out:
                        finish()
                    if n == 0 and s.prep:
                        normalise()
                    if s.prep:
                        if n == 3:
                            convolve(0)
                            convolve(1)
                        if n == 4:
                            silu(0)
                            silu(1)
                            convolve(2)
                            convolve(3)
                            dve.wait_ge(S["conv"], (p + 1) * KE)
                            if s.ph == 0:
                                nc.vector.tensor_copy(pre[:, :, 0:TAPS - 1], pre[:, :, BANK:BANK + TAPS - 1])\
                                    .then_inc(S["history"], 1)
                            else:
                                nc.vector.memset(pre[:, :, 0:TAPS - 1], 0.0).then_inc(S["history"], 1)
                            dve.wait_ge(S["history"], p + 2)
                        if n == 5:
                            silu(2)
                            silu(3)
                        if n == 7:
                            split_c()
                        if n in (10, 11):
                            round_off(n - 10)
                        if n == 14:
                            softplus(0)
                            softplus(1)
                    if s.core and n in (8, 10, 11, 12):
                        gate_skip((8, 10, 11, 12).index(n))

            run(dve, segment)

        @block.tensor
        def _(pe):
            def segment(s):
                i, p = s.i, s.p

                def work(kind, c):
                    place = s.place(kind, c)
                    if not isinstance(place, int) or place > 0:
                        pe.wait_ge(S["work_free"], place)
                    b = bank[6]
                    if kind == "turn":
                        pe.wait_ge(S["xn_tok"], p + 1)
                        for k in range(KD):
                            for t in range(2):
                                op = nc.tensor.transpose(b[:, (2 * k + t) * P:(2 * k + t + 1) * P],
                                                         xn_tok[:, 2 * c + t, k * P:(k + 1) * P], ident[:, :])
                    elif kind in ("in", "skip"):
                        for k in range(KD):
                            o = W256[kind][0] + c * P
                            op = nc.tensor.matmul(b[:, :], w256[:, k, o:o + P],
                                                  xn[:, s.ph if kind == "in" else s.h, k, :],
                                                  start=k == 0, stop=k == KD - 1)
                    elif kind == "xproj":
                        for k in range(KE):
                            pe.wait_ge(S["x"], p * KE + k + 1)
                            op = nc.tensor.matmul(b[0:XROWS, :], col("xproj", k, XROWS), x[:, s.ph, k, :],
                                                  start=k == 0, stop=k == KE - 1)
                    elif kind == "dt":
                        op = nc.tensor.matmul(b[:, :], w64[:, c * P:(c + 1) * P], proj[0:RANK, :],
                                              start=True, stop=True)
                    elif kind == "out":
                        pe.wait_ge(S["y"], i * KE)
                        for t in range(2):
                            for k in range(KE):
                                at = (2 * c + t) * P
                                op = nc.tensor.matmul(b[:, t * DIM:(t + 1) * DIM], gate[:, k, at:at + P],
                                                      col("out", k, DIM), start=k == 0, stop=k == KE - 1)
                    op.then_inc(S["work_done"], 1)

                for n in range(N + 1):
                    j = i * N + n
                    if s.core and n < N:
                        if n == 0:
                            pe.wait_ge(S["parts"], i + 1)
                        if not (s.first and n == 0):
                            pe.wait_ge(S["hc"], 2 * j)
                        nc.tensor.matmul(bank[7][:, :], select[:, n, :], parts[:, s.h, :],
                                         start=True, stop=True).then_inc(S["c_done"], 1)
                    for w in s.at(n, 1):
                        work(*w)
                    if s.core and n > 0:
                        m = n - 1
                        if m == 0 and not s.first:
                            pe.wait_ge(S["y"], i * KE)
                        pe.wait_ge(S["hc"], 2 * j)
                        for c in range(KE):
                            op = nc.tensor.matmul(bank[c][:, :], ident[:, :], hc[:, m % 2, c, :],
                                                  start=m == 0, stop=m == N - 1)
                        op.then_inc(S["y_part"], 1)
                    for w in s.at(n, 2):
                        work(*w)

            run(pe, segment)


def build(nc, x_in, w256_in, w512_in, w128_in, w64_in, out):
    with ExitStack() as ctx:
        sb = lambda n, s, d=F32: ctx.enter_context(nc.sbuf_tensor(n, s, d))
        mem = {
            "x_tok": sb("x_tok", [P, TILES, DIM]),
            "w256": sb("w256", [P, KD, W256_COLS]),
            "w512": sb("w512", [P, KE, W512_COLS]),
            "w128": sb("w128", [P, W128_COLS]),
            "w64": sb("w64", [RANK, W64_COLS]),
            "ident": sb("ident", [P, P]),
            "select": sb("select", [RANK + STATE, STATE, P], BF16),
            "sign": sb("sign", [P, 1]),
            "eps": sb("eps", [P, 1]),
        }
        load_sem = {n: ctx.enter_context(nc.semaphore(f"load_{n}")) for n in ("x", "x0", "x1", "x2", "x3", "weights", "ident", "select")}
        ins = {
            "x": x_in.rearrange("b (t p) d -> p (b t) d", p=P),
            "w256": w256_in.rearrange("(k p) f -> p k f", p=P),
            "w512": w512_in.rearrange("(k p) f -> p k f", p=P),
            "w128": w128_in, "w64": w64_in,
        }
        setup(nc, mem, load_sem, ins)
        ffn(nc, None, mem, "f1", load_sem, None)
        mamba(nc, mem, nc.dram_tensor("b_rows", [2, STATE, BANK], F32, kind="Internal").ap())
        ffn(nc, None, mem, "f2", None, out.rearrange("b (t p) d -> p (b t) d", p=P))


def kernel(**inputs):
    import numpy as np
    import concourse.bacc as bacc
    from concourse.bass_utils import run_bass_kernel_spmd

    a = {n: np.asarray(v) for n, v in inputs.items()}
    f = lambda n: a["L0_ffn_" + n]
    m = lambda n: a["L0_attn_" + n]
    col = lambda v: v.reshape(-1, 1)
    rows = lambda v, n: np.broadcast_to(v.reshape(1, -1), (n, v.size))
    arrays = {
        "x_in": m("resid"),
        "w256_in": np.concatenate([m("in_w").T, m("skip_w").T, f("cn_w1"), f("cn_w2"), f("gc_w1")], axis=1),
        "w512_in": np.concatenate([m("wd1").T, m("wC").T, m("wB").T, m("out_w").T, m("conv_w"), col(m("conv_b")),
                                   col(m("W_D")), col(m("wd2_b")), m("A_log")], axis=1),
        "w128_in": np.concatenate([
            f("cn_w3"), f("gc_w2"), np.broadcast_to(np.concatenate([f("cn_w4")] * 2, axis=0), (P, P)),
            col(f("cn_b2")), col(f("gc_b1")), m("norm_w").reshape(KD, P).T, f("cn_b1").reshape(KD, P).T,
            col(np.concatenate([f("cn_b3")] * 2)), rows(f("cn_b4"), P), rows(f("gc_b3"), P),
            rows(f("adaptive_range"), P)], axis=1),
        "w64_in": np.concatenate([m("wd2").T, np.broadcast_to(f("gc_w3"), (H3, P)), col(f("gc_b2"))], axis=1),
    }
    arrays = {n: np.ascontiguousarray(v) for n, v in arrays.items()}
    nc = bacc.Bacc("TRN2", target_bir_lowering=False, num_devices=1)
    args = [nc.dram_tensor(n, v.shape, mybir.dt.from_np(v.dtype), kind="ExternalInput").ap()
            for n, v in arrays.items()]
    out = nc.dram_tensor("out", arrays["x_in"].shape, F32, kind="ExternalOutput").ap()
    build(nc, *args, out)
    return run_bass_kernel_spmd(nc, [arrays], core_ids=[0]).results[0]["out"]
```

```python
from contextlib import ExitStack

import concourse.bass as bass
from concourse import mybir

F32 = mybir.dt.float32
BF16 = mybir.dt.bfloat16
F32R = mybir.dt.float32r
ALU = mybir.AluOpType
ACT = mybir.ActivationFunctionType
AX = mybir.AxisListType

P = 128
BATCH, SEQ, DIM = 4, 1024, 256
INNER, STATE, RANK, TAPS = 512, 16, 64, 4
EPS = 1e-5
KD = DIM // P
KE = INNER // P
TILES = BATCH * SEQ // P
BT = SEQ // P
BANK = 512
HALVES = SEQ // BANK
XROWS = RANK + 2 * STATE
H3 = 64
CYCLES = 3

W256 = {"in": (0, INNER), "skip": (INNER, INNER), "w1": (2 * INNER, DIM), "w2": (2 * INNER + DIM, P),
        "g1": (2 * INNER + DIM + P, P)}
W256_COLS = 2 * INNER + DIM + 2 * P
W512 = {"xproj": (0, XROWS), "out": (XROWS, DIM), "conv": (XROWS + DIM, TAPS)}
_o = XROWS + DIM + TAPS
W512.update({"conv_b": (_o, 1), "D": (_o + 1, 1), "dt_b": (_o + 2, 1), "A_log": (_o + 3, STATE)})
W512_COLS = _o + 3 + STATE
W128 = {"w3": (0, H3), "g2": (H3, H3), "w4": (2 * H3, P)}
_o = 2 * H3 + P
for _n, _w in (("b2", 1), ("gb1", 1), ("norm", KD), ("b1", KD), ("b3", 1), ("b4", 1), ("gb3", 1), ("ar", 1)):
    W128[_n] = (_o, _w)
    _o += _w
W128_COLS = _o
W64 = {"dt": (0, INNER), "g3": (INNER, P), "gb2": (INNER + P, 1)}
W64_COLS = INNER + P + 1


class Chain:

    def __init__(self, engine, sem):
        self.engine, self.sem, self.count = engine, sem, 0

    def __call__(self, instruction):
        self.count += 1
        instruction.then_inc(self.sem, 1)
        self.engine.wait_ge(self.sem, self.count)


def ffn(nc, mem, name, load_sem, store, measured, measure_next):
    STEPS = CYCLES * BATCH
    HEAD, TAIL = -1, STEPS
    x_tok, w256, w128, w64 = mem["x_tok"], mem["w256"], mem["w128"], mem["w64"]
    ident, sign = mem["ident"], mem["sign"]

    def batch(s):
        return s // (2 * CYCLES) * 2 + s % 2

    def cycle(s):
        return s % (2 * CYCLES) // 2

    WORK = [(HEAD, 0, "in", 0, t) for t in range(BT // 2)]
    WORK += [(0, 0, "in", 1, 0), (0, 1, "in", 1, 1), (0, 2, "in", 1, 2), (0, 3, "in", 1, 3), (0, 3, "g", 0, 0),
             (0, 4, "g", 0, 1), (1, 0, "g", 0, 2)]
    WORK += [(1, 2 + k, "g", 1, k) for k in range(3)]
    WORK += [(2, 1, "in", 2, 0), (2, 3, "in", 2, 1), (3, 1, "in", 2, 2), (3, 3, "in", 2, 3)]
    WORK += [(4, 1, "in", 3, 0), (4, 3, "in", 3, 1), (5, 0, "in", 3, 2), (5, 1, "in", 3, 3)]
    WORK += [(5, 2 + k, "g", 2, k) for k in range(3)]
    WORK += [(6, 0, "back", 0, 0), (6, 1, "back", 0, 1), (6, 4, "back", 0, 2), (7, 0, "back", 0, 3)]
    WORK += [(7, 1 + k, "g", 3, k) for k in range(3)]
    WORK += [(7, 4, "back", 1, 0), (8, 0, "back", 1, 1), (8, 1, "back", 1, 2), (8, 4, "back", 1, 3)]
    WORK += [(11, 4, "back", 2, 0)]
    WORK += [(TAIL, 0, "back", 2, t) for t in range(1, 4)] + [(TAIL, 1, "back", 3, t) for t in range(4)]
    uses = [w[2:] for w in WORK]

    def due(s, place):
        return [w[2:] for w in WORK if w[:2] == (s, place)]

    def bank_of(kind, b, t):
        return t if (kind, b) in (("in", 0), ("back", 2), ("back", 3)) and (b, t) != (2, 0) else 7

    with ExitStack() as ctx:
        sb = lambda n, s, d=F32: ctx.enter_context(nc.sbuf_tensor(f"{name}_{n}", s, d))
        sem = lambda n: ctx.enter_context(nc.semaphore(f"{name}_{n}"))
        bank = [ctx.enter_context(nc.psum_tensor(f"{name}_bank{i}", [P, BANK], F32)) for i in range(8)]
        stats = sb("stats", [P, TILES, 6])
        moments = mem["moments"]
        std = sb("std", [P, TILES])
        rstd = sb("rstd", [P, TILES])
        z_tok = sb("z_tok", [P, 4, DIM])
        state = sb("state", [P, KD, BATCH * SEQ])
        state_hi = sb("state_hi", [P, KD, BATCH * SEQ], F32R)
        state_lo = sb("state_lo", [P, KD, BATCH * SEQ], F32R)
        w1_hi = sb("w1_hi", [P, KD, DIM], F32R)
        w1_lo = sb("w1_lo", [P, KD, DIM], F32R)
        total = sb("total", [P, KD, BATCH])
        g1 = sb("g1", [P, BATCH])
        g2 = sb("g2", [H3, BATCH])
        gt = sb("gt", [P, BATCH])
        constant = sb("constant", [P, BATCH])
        shifted = sb("shifted", [P, BATCH])
        base = sb("base", [P, BATCH])
        slope = sb("slope", [P, 1])
        half_b4 = sb("half_b4", [P, 2])
        h1 = sb("h1", [P, KD, SEQ])
        h2 = sb("h2", [P, SEQ])
        h3 = sb("h3", [P, BANK])
        th = sb("th", [P, SEQ])
        couple = sb("couple", [P, SEQ])
        turned = sb("turned", [P, KD, SEQ])

        stats_ready, moments_ready, std_ready, rstd_ready = sem("stats"), sem("moments"), sem("std"), sem("rstd")
        z_ready, total_ready, base_ready, constants = sem("z"), sem("total"), sem("base"), sem("constants")
        work_done, work_read, back_added = sem("work_done"), sem("work_read"), sem("added")
        l1_done, l2_done, l3_done, l4_done = sem("l1"), sem("l2"), sem("l3"), sem("l4")
        h1_ready, h2_ready, h3_ready, th_ready = sem("h1r"), sem("h2r"), sem("h3r"), sem("thr")
        updated, stored = sem("updated"), sem("stored")
        w1_split, rounded, split = sem("w1_split"), sem("rounded"), sem("split")
        block = ctx.enter_context(nc.Block())

        def w(t, table, key, k=None):
            o, n = table[key]
            return t[:, k, o:o + n] if k is not None else t[:, o:o + n]

        def done_count(use):
            return uses.index(use) + 1

        def wait_read(engine, use):
            before = uses[:uses.index(use) + 1]
            backs = sum(u[0] == "back" for u in before)
            if use[0] == "back":
                engine.wait_ge(back_added, backs)
            else:
                engine.wait_ge(work_read, len(before) - backs)

        def updates(s, h):
            return (s * HALVES + h + 1) * 5

        SPLITS = [("in", 0, t) for t in range(4)] + [("in", 1, t) for t in range(4)]
        for s in range(STEPS):
            if cycle(s) < CYCLES - 1:
                SPLITS += [("update", s, h) for h in range(HALVES)]
            SPLITS += [u for k in range(5) for u in due(s, k) if u[0] == "in" and u[1] > 1]

        def split_columns(job):
            kind, a, i = job
            o = a * SEQ + 2 * i * P if kind == "in" else batch(a) * SEQ + i * BANK
            return slice(o, o + (2 * P if kind == "in" else BANK))

        @block.gpsimd
        def _(pool):
            for n, job in enumerate(SPLITS):
                cs = split_columns(job)
                pool.wait_ge(rounded, n + 1)
                nc.gpsimd.tensor_tensor(state_lo[:, :, cs], state[:, :, cs], state_hi[:, :, cs].bitcast(F32),
                                        ALU.subtract).then_inc(split, 1)

        @block.vector
        def _(dve):
            chain = Chain(dve, base_ready)

            def round_state(*job):
                cs = split_columns(job)
                if job[0] == "in":
                    wait_read(dve, job)
                else:
                    dve.wait_ge(updated, updates(*job[1:]))
                nc.vector.tensor_copy(state_hi[:, :, cs], state[:, :, cs]).then_inc(rounded, 1)


            def moments_of(batches):
                if batches[0] in measured:
                    return
                for b in batches:
                    if load_sem is not None:
                        dve.wait_ge(load_sem["x"], b + 1)
                    for t in range(b * BT, (b + 1) * BT):
                        last = nc.vector.bn_stats(stats[:, t, :], x_tok[:, t, :])
                last.then_inc(stats_ready, 1)
                dve.wait_ge(stats_ready, stats_count[batches] - len(measured))
                for b in batches:
                    for t in range(b * BT, (b + 1) * BT):
                        last = nc.vector.bn_aggr(moments[:, t, :], stats[:, t, :])
                last.then_inc(moments_ready, 1)

            stats_count = {(0,): 1, (1,): 2, (2, 3): 3}

            def invert(batches):
                ts = slice(batches[0] * BT, (batches[-1] + 1) * BT)
                dve.wait_ge(std_ready, stats_count[batches])
                nc.vector.reciprocal(rstd[:, ts], std[:, ts]).then_inc(rstd_ready, 1)
                dve.wait_ge(rstd_ready, stats_count[batches])

            def normalise(b, t):
                o = b * BT + 2 * t
                if (b, t) >= (0, 2):
                    earlier = (b, t - 2) if t >= 2 else (b - 1, t + 2)
                    dve.wait_ge(work_done, done_count(("in",) + earlier))
                for i in range(2):
                    last = nc.vector.tensor_scalar(z_tok[:, (2 * t + i) % 4, :], x_tok[:, o + i, :],
                                                   moments[:, o + i, 0:1], rstd[:, o + i:o + i + 1],
                                                   ALU.subtract, ALU.mult)
                last.then_inc(z_ready, 1)

            def sum_up(b):
                wait_read(dve, ("in", b, 3))
                nc.vector.tensor_reduce(total[:, :, b:b + 1], state[:, :, b * SEQ:(b + 1) * SEQ].unsqueeze(2),
                                        AX.X, ALU.add).then_inc(total_ready, 1)

            def coupling_base(b):
                wait_read(dve, ("g", b, 2))
                one = slice(b, b + 1)
                chain(nc.vector.tensor_scalar(constant[:, one], gt[:, one], w(w128, W128, "ar"), 0.7,
                                              ALU.mult, ALU.mult))
                chain(nc.vector.tensor_scalar(shifted[:, one], constant[:, one], 0.1, None, ALU.add))
                chain(nc.vector.tensor_scalar(base[:, one], shifted[:, one], sign[:, 0:1], None, ALU.mult))

            def update(s, h):
                b = batch(s)
                c = slice(h * BANK, (h + 1) * BANK)
                cs = slice(b * SEQ + h * BANK, b * SEQ + (h + 1) * BANK)
                before = updates(s, h) - 5
                dve.wait_ge(th_ready, s * HALVES + h + 1)
                nc.vector.tensor_scalar(couple[:, c], th[:, c], slope[:, 0:1], base[:, b:b + 1], ALU.mult, ALU.add)\
                    .then_inc(updated, 1)
                dve.wait_ge(updated, before + 1)
                nc.vector.tensor_tensor(turned[:, 0, c], couple[:, c], state[:, 1, cs], ALU.mult)\
                    .then_inc(updated, 1)
                nc.vector.tensor_tensor(turned[:, 1, c], couple[:, c], state[:, 0, cs], ALU.mult)\
                    .then_inc(updated, 1)
                dve.wait_ge(updated, before + 3)
                nc.vector.tensor_tensor(state[:, 0, cs], state[:, 0, cs], turned[:, 0, c], ALU.add)\
                    .then_inc(updated, 1)
                nc.vector.tensor_tensor(state[:, 1, cs], state[:, 1, cs], turned[:, 1, c], ALU.subtract)\
                    .then_inc(updated, 1)

            def add_back(b, t):
                use = ("back", b, t)
                dve.wait_ge(work_done, done_count(use))
                tiles = x_tok[:, b * BT + 2 * t:b * BT + 2 * t + 2, :]
                nc.vector.scalar_tensor_tensor(tiles, bank[bank_of(*use)][:, :].rearrange("p (a d) -> p a d", a=2),
                                               0.5, tiles, ALU.mult, ALU.add).then_inc(back_added, 1)

            def measure(b):
                dve.wait_ge(back_added, b * 4 + 4)
                for t in range(b * BT, (b + 1) * BT):
                    last = nc.vector.bn_stats(stats[:, t, :], x_tok[:, t, :])
                last.then_inc(stats_ready, 1)
                dve.wait_ge(stats_ready, 4 + b)
                for t in range(b * BT, (b + 1) * BT):
                    nc.vector.bn_aggr(moments[:, t, :], stats[:, t, :])

            def split_w1():
                if load_sem is not None:
                    dve.wait_ge(load_sem["weights"], 48)
                w1 = w(w256, W256, "w1", slice(0, KD))
                nc.vector.tensor_copy(w1_hi[:, :, :], w1).then_inc(w1_split, 1)
                dve.wait_ge(w1_split, 1)
                nc.vector.tensor_tensor(w1_lo[:, :, :], w1, w1_hi[:, :, :].bitcast(F32), ALU.subtract)\
                    .then_inc(w1_split, 1)

            moments_of((0,))
            if load_sem is None:
                split_w1()
            invert((0,))
            for t in range(4):
                normalise(0, t)
            if load_sem is not None:
                split_w1()
            for t in range(4):
                round_state("in", 0, t)
            moments_of((1,))
            invert((1,))
            normalise(1, 0)
            normalise(1, 1)
            sum_up(0)
            normalise(1, 2)
            normalise(1, 3)
            for t in range(4):
                round_state("in", 1, t)
            nc.vector.tensor_scalar(half_b4[:, 0:1], w(w128, W128, "b4"), 0.5, None, ALU.mult)
            nc.vector.tensor_scalar(half_b4[:, 1:2], w(w128, W128, "gb3"), 0.5, None, ALU.mult)
            nc.vector.tensor_scalar(slope[:, :], w(w128, W128, "ar"), sign[:, 0:1], 0.3, ALU.mult, ALU.mult)\
                .then_inc(constants, 1)
            dve.wait_ge(constants, 1)
            moments_of((2, 3))
            sum_up(1)
            coupling_base(0)
            def adds(s, places):
                for place in places:
                    for kind, b, t in due(s, place):
                        if kind == "back":
                            add_back(b, t)

            for s in range(STEPS + 1):
                adds(s, (0,) if s == TAIL else (0, 1))
                if s == TAIL and measure_next:
                    measure(2)
                if s > 0:
                    for h in range(HALVES):
                        update(s - 1, h)
                        if cycle(s - 1) < CYCLES - 1:
                            round_state("update", s - 1, h)
                    for kind, b, t in [u for k in range(5) for u in due(s - 1, k)]:
                        if kind == "in" and b > 1:
                            round_state("in", b, t)
                if s == 1:
                    invert((2, 3))
                    coupling_base(1)
                if s in (1, 2, 3, 4):
                    for t in range(2):
                        normalise(2 + (s - 1) // 2, 2 * ((s - 1) % 2) + t)
                if s == 4:
                    sum_up(2)
                if s == 5:
                    sum_up(3)
                if s == 6:
                    coupling_base(2)
                if s == 7:
                    coupling_base(3)
                if s in (9, 10) and measure_next:
                    measure(s - 9)
                if s < TAIL:
                    adds(s, (4,))
            for t in range(4):
                add_back(3, t)
            if measure_next:
                measure(3)

        @block.tensor
        def _(pe):
            def layer1(s, h, m):
                b = batch(s)
                if s > 0:
                    pe.wait_ge(h1_ready, (s - 1) * 4 + h * 2 + m + 1)
                job = ("in", b, 2 * h + 1) if cycle(s) == 0 else ("update", s - 2, h)
                pe.wait_ge(split, SPLITS.index(job) + 1)
                cs = slice(b * SEQ + h * BANK, b * SEQ + (h + 1) * BANK)
                passes = [(k, wt, st) for k in range(KD)
                          for wt, st in ((w1_lo, state_hi), (w1_hi, state_lo), (w1_hi, state_hi))]
                for n, (k, wt, st) in enumerate(passes):
                    last = nc.tensor.matmul(bank[h * 2 + m][:, :], wt[:, k, m * P:(m + 1) * P], st[:, k, cs],
                                            start=n == 0, stop=n == len(passes) - 1)
                last.then_inc(l1_done, 1)

            def layer2(s, h):
                pe.wait_ge(h1_ready, s * 4 + h * 2 + 2)
                if s > 0 and h == 0:
                    pe.wait_ge(th_ready, s * HALVES)
                if s > 0 and h == 1:
                    pe.wait_ge(h2_ready, s * HALVES)
                for k in range(KD):
                    last = nc.tensor.matmul(bank[4 + h][:, :], w(w256, W256, "w2", k),
                                            h1[:, k, h * BANK:(h + 1) * BANK], start=k == 0, stop=k == KD - 1)
                last.then_inc(l2_done, 1)

            def layer3(s):
                pe.wait_ge(h2_ready, s * HALVES + 2)
                if s > 0:
                    pe.wait_ge(th_ready, s * HALVES - 1)
                for h in range(HALVES):
                    last = nc.tensor.matmul(bank[6][h * H3:(h + 1) * H3, :], w(w128, W128, "w3"),
                                            h2[:, h * BANK:(h + 1) * BANK], start=True, stop=True)
                last.then_inc(l3_done, 1)

            def layer4(s):
                pe.wait_ge(h3_ready, s + 1)
                for h in range(HALVES):
                    o = W128["w4"][0]
                    nc.tensor.matmul(bank[6 if h == 0 else 4][:, :], w128[h * H3:(h + 1) * H3, o:o + P],
                                     h3[h * H3:(h + 1) * H3, :], start=True, stop=True).then_inc(l4_done, 1)

            def work(use):
                kind, b, t = use
                at = uses.index(use)
                earlier = [u for u in uses[:at] if bank_of(*u) == bank_of(*use)]
                if earlier:
                    wait_read(pe, earlier[-1])
                out = bank[bank_of(*use)]
                if kind == "in":
                    pe.wait_ge(z_ready, b * (BT // 2) + t + 1)
                    for k in range(KD):
                        for i in range(2):
                            last = nc.tensor.transpose(out[:, (2 * k + i) * P:(2 * k + i + 1) * P],
                                                       z_tok[:, (2 * t + i) % 4, k * P:(k + 1) * P], ident[:, :])
                elif kind == "back":
                    pe.wait_ge(updated, updates(max(s for s in range(STEPS) if batch(s) == b), t // 2))
                    for i in range(2):
                        for k in range(KD):
                            o = b * SEQ + (2 * t + i) * P
                            last = nc.tensor.transpose(out[:, (i * KD + k) * P:(i * KD + k + 1) * P],
                                                       state[:, k, o:o + P], ident[:, :])
                elif t == 0:
                    pe.wait_ge(total_ready, b + 1)
                    for k in range(KD):
                        last = nc.tensor.matmul(out[:, 0:1], w(w256, W256, "g1", k), total[:, k, b:b + 1],
                                                start=k == 0, stop=k == KD - 1)
                else:
                    wait_read(pe, ("g", b, t - 1))
                    if t == 1:
                        last = nc.tensor.matmul(out[0:H3, 0:1], w(w128, W128, "g2"), g1[:, b:b + 1],
                                                start=True, stop=True)
                    else:
                        last = nc.tensor.matmul(out[:, 0:1], w(w64, W64, "g3"), g2[:, b:b + 1], start=True, stop=True)
                last.then_inc(work_done, 1)

            def side(s, place):
                for use in due(s, place):
                    work(use)

            if load_sem is not None:
                pe.wait_ge(load_sem["ident"], 2)
            side(HEAD, 0)
            if load_sem is not None:
                pe.wait_ge(load_sem["weights"], 48)
            pe.wait_ge(w1_split, 2)
            for s in range(STEPS):
                layer1(s, 0, 0)
                if s > 0:
                    layer3(s - 1)
                side(s, 0)
                layer1(s, 0, 1)
                if s > 0:
                    layer4(s - 1)
                side(s, 1)
                layer1(s, 1, 0)
                side(s, 2)
                layer1(s, 1, 1)
                side(s, 3)
                layer2(s, 0)
                side(s, 4)
                layer2(s, 1)
            layer3(STEPS - 1)
            side(TAIL, 0)
            layer4(STEPS - 1)
            side(TAIL, 1)

        @block.scalar
        def _(act):
            def deviation(batches, count):
                ts = slice(batches[0] * BT, (batches[-1] + 1) * BT)
                if batches[0] not in measured:
                    act.wait_ge(moments_ready, count - len(measured))
                nc.scalar.activation(std[:, ts], moments[:, ts, 1], ACT.Sqrt, bias=mem["eps"][:, 0:1])\
                    .then_inc(std_ready, 1)

            def gelu1(s, h, m):
                act.wait_ge(l1_done, s * 4 + h * 2 + m + 1)
                o = W128["b1"][0] + m
                nc.scalar.activation(h1[:, m, h * BANK:(h + 1) * BANK], bank[h * 2 + m][:, :], ACT.Gelu,
                                     bias=w128[:, o:o + 1]).then_inc(h1_ready, 1)

            def gelu2(s, h):
                act.wait_ge(l2_done, s * HALVES + h + 1)
                nc.scalar.activation(h2[:, h * BANK:(h + 1) * BANK], bank[4 + h][:, :], ACT.Gelu,
                                     bias=w(w128, W128, "b2")).then_inc(h2_ready, 1)

            def gelu3(s):
                act.wait_ge(l3_done, s + 1)
                nc.scalar.activation(h3[:, :], bank[6][:, :], ACT.Gelu, bias=w(w128, W128, "b3"))\
                    .then_inc(h3_ready, 1)

            def tanh4(s, h):
                act.wait_ge(l4_done, s * HALVES + h + 1)
                if s > 0:
                    act.wait_ge(updated, updates(s - 1, h))
                nc.scalar.activation(th[:, h * BANK:(h + 1) * BANK], bank[6 if h == 0 else 4][:, :], ACT.Tanh,
                                     bias=half_b4[:, 0:1], scale=0.5).then_inc(th_ready, 1)

            def read(s, place):
                for use in due(s, place):
                    kind, b, t = use
                    if kind == "back":
                        continue
                    act.wait_ge(work_done, done_count(use))
                    source, one = bank[bank_of(*use)], slice(b, b + 1)
                    if kind == "in":
                        o = b * SEQ + 2 * t * P
                        op = nc.scalar.activation(state[:, :, o:o + 2 * P],
                                                  source[:, :].rearrange("p (k n) -> p k n", k=KD), ACT.Copy)
                    elif t == 0:
                        op = nc.scalar.activation(g1[:, one], source[:, 0:1], ACT.Gelu, bias=w(w128, W128, "gb1"),
                                                  scale=1.0 / SEQ)
                    elif t == 1:
                        op = nc.scalar.activation(g2[:, one], source[0:H3, 0:1], ACT.Gelu,
                                                  bias=w64[:, W64["gb2"][0]:][:, 0:1])
                    else:
                        act.wait_ge(constants, 1)
                        op = nc.scalar.activation(gt[:, one], source[:, 0:1], ACT.Tanh, bias=half_b4[:, 1:2],
                                                  scale=0.5)
                    op.then_inc(work_read, 1)

            deviation((0,), 1)
            read(HEAD, 0)
            deviation((1,), 2)
            if load_sem is not None:
                act.wait_ge(load_sem["weights"], 48)
            for s in range(STEPS):
                gelu1(s, 0, 0)
                if s > 0:
                    gelu3(s - 1)
                read(s, 0)
                gelu1(s, 0, 1)
                if s > 0:
                    tanh4(s - 1, 0)
                    tanh4(s - 1, 1)
                read(s, 1)
                if s == 1:
                    deviation((2, 3), 3)
                gelu1(s, 1, 0)
                read(s, 2)
                gelu1(s, 1, 1)
                read(s, 3)
                gelu2(s, 0)
                read(s, 4)
                gelu2(s, 1)
            gelu3(STEPS - 1)
            tanh4(STEPS - 1, 0)
            tanh4(STEPS - 1, 1)

        if load_sem is not None:
            @block.sync
            def _(sp):
                for b in range(BATCH):
                    sp.wait_ge(load_sem[f"x{b}"], 16)
                    sp.sem_inc(load_sem["x"], 1)
                sp.wait_ge(load_sem["late_weights"], 32)

        if store is not None:
            @block.sync
            def _(sp):
                stores = [(b, 0, BT) for b in range(BATCH - 1)] + [(BATCH - 1, 0, BT // 2), (BATCH - 1, BT // 2, BT)]
                for b, lo, hi in stores:
                    wait_read(sp, ("back", b, hi // 2 - 1))
                    ts = slice(b * BT + lo, b * BT + hi)
                    sp.dma_start(store[:, ts, :], x_tok[:, ts, :]).then_inc(stored, 16)
                sp.wait_ge(stored, len(stores) * 16)


def setup(nc, mem, load_sem, ins):
    x_tok = mem["x_tok"]
    with nc.Block() as block:
        first = 2 * INNER

        @block.sync
        def _(sp):
            for b in range(BATCH):
                if b == 1:
                    sp.wait_ge(load_sem["weights"], 48)
                sp.dma_start(x_tok[:, b * BT:(b + 1) * BT, :], ins["x"][:, b * BT:(b + 1) * BT, :])\
                    .then_inc(load_sem[f"x{b}"], 16)
            sp.dma_start(mem["w256"][:, :, :first], ins["w256"][:, :, :first]).then_inc(load_sem["late_weights"], 16)
            sp.dma_start(mem["w512"][...], ins["w512"]).then_inc(load_sem["late_weights"], 16)

        @block.scalar
        def _(act):
            act.dma_start(mem["w256"][:, :, first:], ins["w256"][:, :, first:]).then_inc(load_sem["weights"], 16)
            for n in ("w128", "w64"):
                act.dma_start(mem[n][...], ins[n]).then_inc(load_sem["weights"], 16)

        @block.vector
        def _(dve):
            nc.vector.memset(mem["eps"][:, :], EPS)
            nc.vector.memset(mem["sign"][0:H3, :], 1.0)
            nc.vector.memset(mem["sign"][H3:P, :], -1.0)

        @block.gpsimd
        def _(pool):
            nc.gpsimd.memset(mem["ident"][:, :], 0.0).then_inc(load_sem["ident"], 1)
            nc.gpsimd.memset(mem["select"][:, :, :], 0.0).then_inc(load_sem["select"], 1)
            pool.wait_ge(load_sem["ident"], 1)
            nc.gpsimd.affine_select(out=mem["ident"][:, :], in_=mem["ident"][:, :], compare_op=ALU.not_equal,
                                    fill=1.0, base=0, pattern=[[-1, P]], channel_multiplier=1)\
                .then_inc(load_sem["ident"], 1)
            for a in range(3):
                pool.wait_ge(load_sem["select"], a + 1)
                nc.gpsimd.affine_select(out=mem["select"][:, :, :], in_=mem["select"][:, :, :],
                                        compare_op=ALU.not_equal, fill=1.0, base=-32 * a,
                                        pattern=[[-1, STATE], [0, P]], channel_multiplier=1)\
                    .then_inc(load_sem["select"], 1)


def mamba(nc, mem, b_rows):
    x_tok, w256, w512, w64, w128 = mem["x_tok"], mem["w256"], mem["w512"], mem["w64"], mem["w128"]
    ident, select, eps = mem["ident"], mem["select"], mem["eps"]
    HT = BANK // P
    SEGS = BATCH * HALVES
    N = STATE
    PARTS = {"out": 2, "turn": 1, "in": 2, "xproj": 2, "dt": 1, "skip": 2}
    PLACES = {
        "out": ((3, 2), (3, 2), (4, 2), (4, 2)),
        "turn": ((0, 1), (0, 1)),
        "in": ((1, 1), (1, 1), (2, 2), (2, 2), (2, 2), (2, 2), (4, 1), (4, 1)),
        "xproj": ((5, 2), (5, 2)),
        "dt": ((7, 1), (7, 2), (8, 1), (8, 2)),
        "skip": ((10, 1), (10, 1), (10, 2), (10, 2), (12, 2), (12, 2), (13, 2), (13, 2)),
    }
    PLAN = sorted(((step, place, kind, j // PARTS[kind], j % PARTS[kind])
                   for kind in PLACES for j, (step, place) in enumerate(PLACES[kind])),
                  key=lambda w: (w[0], w[1], list(PLACES).index(w[2]), w[3], w[4]))

    AT = {
        "z": (5,),
        "conv": (7, 8, 9, 12),
        "tanh_x": (9, 9, 11, 13),
        "silu": (9, 9, 11, 13),
        "split": (15, 18),
        "mid": (16,),
        "abs": (19, 19, 19, 20),
        "exp": (19, 20, 20, 22),
        "add1": (19, 20, 21, 22),
        "corr": (22, 22),
        "ln": (23, 25),
        "softplus": (25, 28),
        "gate": (23, 25, 31, 33),
        "log1p": (13, 13),
        "dx": (14, 16),
        "z_add": (3,),
        "out_add": (6, 7),
    }

    def due(time, kind):
        return [c for c, t in enumerate(AT[kind]) if t == time]

    class Segment:

        def __init__(self, i, parity, core=True, prep=True, out=True, base=None, first=False):
            self.i, self.h, self.core, self.prep, self.out, self.first = i, parity, core, prep, out, first
            self.p = i + 1
            self.ph = 1 - parity
            kinds = {"turn": prep, "in": prep, "xproj": prep, "dt": prep, "skip": core, "out": out}
            self.plan = [w for w in PLAN if kinds[w[2]]]
            self.base = base
            self.uses = [w[2:4] for w in self.plan if w[4] == 0]

        def place(self, kind, c):
            return self.base + self.uses.index((kind, c))

        def at(self, n, slot):
            return [w[2:] for w in self.plan if w[0] == n and w[1] == slot]

        def finished(self, n, slot):
            return [w[:2] for w in self.at(n, slot) if w[2] == PARTS[w[0]] - 1]

    FULL = len([w for w in PLAN if w[4] == 0])
    prologue = Segment(-1, 1, core=False, out=False, base=0)
    head = Segment(0, 0, out=False, base=len(prologue.uses), first=True)
    after_head = head.base + len(head.uses)
    last = Segment(SEGS - 1, 1, prep=False, base=after_head + FULL * (SEGS - 2))
    tail = Segment(SEGS, 0, core=False, prep=False, base=last.base + len(last.uses))

    def middle(k):
        return [Segment(2 * k + 1 + d, 1 - d, base=after_head + FULL * (2 * k + d)) for d in range(2)]

    def run(engine, segment):
        segment(prologue)
        segment(head)
        with engine.Fori(0, (SEGS - 2) // 2) as k:
            for s in middle(k):
                segment(s)
        segment(last)
        segment(tail)

    with ExitStack() as ctx:
        sb = lambda n, s, d=F32: ctx.enter_context(nc.sbuf_tensor(f"m_{n}", s, d))
        sem = lambda n: ctx.enter_context(nc.semaphore(f"m_{n}"))
        bank = [ctx.enter_context(nc.psum_tensor(f"m_bank{i}", [P, BANK], F32)) for i in range(8)]
        moments = mem["moments"]
        root = sb("root", [P, TILES])
        square = sb("square", [P, TILES])
        rstd = sb("rstd", [P, TILES])
        rrms = sb("rrms", [P, TILES])
        shift = sb("shift", [P, TILES])
        scale_n = sb("scale_n", [P, TILES])
        shift_n = sb("shift_n", [P, TILES])
        xn = sb("xn", [P, 2, KD, BANK])
        negA = sb("negA", [P, KE, STATE])
        expA = sb("expA", [P, KE, STATE])
        diag_d = sb("diag_d", [P, KE, P])
        one = sb("one", [P, 1])
        conv = sb("conv", [P, KE, TAPS + 1])
        pre = sb("pre", [P, KE, TAPS - 1 + BANK])
        th = sb("th", [P, 2, BANK])
        gate = sb("gate", [P, KE, BANK])
        x = sb("x", [P, 2, KE, BANK])
        proj = sb("proj", [XROWS, BANK])
        parts = sb("parts", [RANK + STATE, 2, BANK], BF16)
        tmp_u = sb("tmp_u", [P, KE, BANK])
        delta = sb("delta", [P, 2, KE, BANK])
        dx = sb("dx", [P, 2, KE, BANK])
        brow = sb("brow", [P, 2, 2, BANK])
        u = sb("u", [P, 2, KE, BANK])
        hid = sb("hid", [P, 2, KE, BANK])
        carry = sb("carry", [P, STATE, KE])
        hc = sb("hc", [P, 2, KE, BANK])
        xn_tok = tmp_u[:, 0:2, :].rearrange("p a (b d) -> p (a b) d", d=DIM)
        z_tok = tmp_u[:, 2:4, :].rearrange("p a (b d) -> p (a b) d", d=DIM)
        acc, th_x = dx, tmp_u
        final_stats = tmp_u[:, 0, 0:2 * BT * 6].rearrange("p (t s) -> p t s", s=6)
        rest = [dx[0:RANK + STATE, a, 0] for a in range(2)]
        mid = [dx[0:RANK + STATE, a, 1].bitcast(BF16)[:, 0:BANK] for a in range(2)]

        S = {n: sem(n) for n in (
            "negA", "root", "final_stats", "square", "rstd", "z", "xn_tok", "z_added", "work_done", "work_free",
            "history", "taps", "conv", "tanh_x", "x", "gate", "parts", "rest", "mid", "abs", "e", "u1", "corr",
            "ln", "log1p", "delta", "dx", "b_stored", "b_there", "brow0", "brow1", "u", "a", "scan", "carry",
            "c_done", "hc", "y_part", "diag_d", "y", "out_added", "expA", "zeroed")}
        block = ctx.enter_context(nc.Block())

        def work_bank(s, kind, c):
            return bank[c] if s.prep and not s.core and kind != "xproj" else bank[6]

        def col(key, c, n=1):
            o = W512[key][0]
            return w512[:, c, o:o + n]

        @block.sync
        def _(sp):
            def segment(s):
                def load(i, h, q, fresh=False):
                    if not fresh:
                        sp.wait_ge(S["u"], i * N + 2 * q - 2)
                    sp.dma_start(brow[:, q % 2, :, :],
                                 b_rows[h, 2 * q:2 * q + 2, :].unsqueeze(0).to_broadcast([P, 2, BANK]))\
                        .then_inc(S[f"brow{q % 2}"], 16)

                if s.core:
                    for q in range(2, 7):
                        load(s.i, s.h, q)
                if s.prep:
                    sp.wait_ge(S["work_free"], s.place("xproj", 0) + 1)
                    sp.dma_start(b_rows[s.ph], proj[RANK + STATE:XROWS, :]).then_inc(S["b_stored"], 16)
                if s.core:
                    load(s.i, s.h, 7)
                if s.prep:
                    sp.wait_ge(S["b_stored"], 16 * (s.p + 1))
                    sp.sem_inc(S["b_there"], 1)
                    load(s.p, s.ph, 0, fresh=not s.core)
                    load(s.p, s.ph, 1, fresh=not s.core)

            run(sp, segment)

        @block.scalar
        def _(act):
            nc.scalar.activation(root[:, :], moments[:, :, 1], ACT.Sqrt, bias=eps[:, 0:1]).then_inc(S["root"], 1)
            act.wait_ge(S["square"], 2)
            nc.scalar.activation(root[:, :], square[:, :], ACT.Sqrt, bias=eps[:, 0:1]).then_inc(S["root"], 1)
            o = W512["A_log"][0]
            nc.scalar.activation(expA[:, :, :], w512[:, :, o:o + STATE], ACT.Exp).then_inc(S["expA"], 1)
            act.wait_ge(S["expA"], 1)
            nc.scalar.mul(negA[:, :, :], expA[:, :, :], -1.0).then_inc(S["negA"], 1)
            act.wait_ge(S["negA"], 1)

            def segment(s):
                i, p = s.i, s.p

                def decay(n, c):
                    j = i * N + n
                    if not (s.first and n == 0 and c < 2):
                        act.wait_ge(S["scan"], j * KE + c - 1)
                    nc.scalar.activation(bank[4 + c % 2][:, :], delta[:, s.h, c, :], ACT.Exp,
                                         scale=negA[:, c, n:n + 1]).then_inc(S["a"], 1)

                def evacuate(kind, c):
                    act.wait_ge(S["work_done"], s.place(kind, c) + 1)
                    b = work_bank(s, kind, c)
                    if kind == "turn":
                        for k in range(KD):
                            o = W128["norm"][0] + k
                            op = nc.scalar.activation(xn[:, s.ph, k, c * 2 * P:(c + 1) * 2 * P],
                                                      b[:, k * 2 * P:(k + 1) * 2 * P], ACT.Copy,
                                                      scale=w128[:, o:o + 1])
                    elif kind == "in":
                        act.wait_ge(S["history"], p + 1)
                        if s.core and not s.first:
                            act.wait_ge(S["u"], i * N)
                        nc.scalar.activation(pre[:, c, TAPS - 1:TAPS - 1 + BANK], b[:, :], ACT.Copy)
                        op = nc.scalar.activation(acc[:, s.ph, c, :], b[:, :], ACT.Identity,
                                                  scale=conv[:, c, TAPS - 1:TAPS], bias=conv[:, c, TAPS:TAPS + 1])
                    elif kind == "skip":
                        if c == 0 and not s.first:
                            act.wait_ge(S["out_added"], 2 * i)
                        if c >= 2:
                            act.wait_ge(S["gate"], i * KE + c - 1)
                        nc.scalar.activation(th[:, c % 2, :], b[:, :], ACT.Tanh, scale=0.5)
                        op = nc.scalar.activation(gate[:, c, :], b[:, :], ACT.Copy)
                    elif kind == "xproj":
                        if s.core:
                            act.wait_ge(S["b_stored"], 16 * p)
                            act.wait_ge(S["parts"], p)
                        nc.scalar.activation(parts[RANK:RANK + STATE, s.ph, :], b[RANK:RANK + STATE, :], ACT.Copy)
                        op = nc.scalar.activation(proj[:, :], b[0:XROWS, :], ACT.Copy)
                    elif kind == "dt":
                        op = nc.scalar.activation(delta[:, s.ph, c, :], b[:, :], ACT.Identity, bias=col("dt_b", c))
                    elif kind == "out":
                        act.wait_ge(S["gate"], i * KE)
                        op = nc.scalar.activation(th[:, c, :], b[:, :], ACT.Copy)
                    op.then_inc(S["work_free"], 1)

                def standardise(to, scale, bias, signal):
                    for t in range(HT):
                        one_tile = x_tok[:, bass.ds(p * HT + t, 1), :].rearrange("p a d -> p (a d)") \
                            if not isinstance(p, int) else x_tok[:, p * HT + t, :]
                        op = nc.scalar.activation(to[:, t, :], one_tile, ACT.Identity,
                                                  scale=scale[:, bass.ds(p * HT + t, 1)],
                                                  bias=bias[:, bass.ds(p * HT + t, 1)])
                    op.then_inc(S[signal], 1)

                def side(time):
                    if not s.prep:
                        return
                    if due(time, "z"):
                        standardise(z_tok, rstd, shift, "z")
                    if due(time, "mid"):
                        R = slice(RANK, RANK + STATE)
                        act.wait_ge(S["rest"], p + 1)
                        nc.scalar.activation(mid[s.ph][R, :], rest[s.ph][R, :], ACT.Copy)
                        nc.scalar.activation(parts[0:STATE, s.ph, :], rest[s.ph][R, :], ACT.Copy)\
                            .then_inc(S["mid"], 1)
                    for c in due(time, "tanh_x"):
                        act.wait_ge(S["conv"], p * KE + c + 1)
                        if c == 2:
                            act.wait_ge(S["z_added"], p + 1)
                        nc.scalar.activation(th_x[:, c, :], acc[:, s.ph, c, :], ACT.Tanh).then_inc(S["tanh_x"], 1)
                    for c in due(time, "abs"):
                        act.wait_ge(S["work_free"], s.place("dt", c) + 1)
                        act.wait_ge(S["x"], (p + 1) * KE)
                        act.wait_ge(S["parts"], p + 1)
                        nc.scalar.activation(dx[:, s.ph, c], delta[:, s.ph, c], ACT.Abs).then_inc(S["abs"], 1)
                    for c in due(time, "exp"):
                        act.wait_ge(S["abs"], p * KE + c + 1)
                        nc.scalar.activation(dx[:, s.ph, c], dx[:, s.ph, c], ACT.Exp, scale=-1.0).then_inc(S["e"], 1)
                    for c in due(time, "add1"):
                        act.wait_ge(S["e"], p * KE + c + 1)
                        nc.scalar.activation(tmp_u[:, c], dx[:, s.ph, c], ACT.Identity, bias=one[:, 0:1])\
                            .then_inc(S["u1"], 1)
                    for g in due(time, "ln"):
                        cs = slice(2 * g, 2 * g + 2)
                        act.wait_ge(S["corr"], 2 * p + g + 1)
                        nc.scalar.activation(tmp_u[:, cs], tmp_u[:, cs], ACT.Ln).then_inc(S["ln"], 1)

                for n in range(N + 1):
                    if s.core and n < N:
                        if n == 0:
                            act.wait_ge(S["delta"], 2 * (i + 1))
                        decay(n, 0)
                        decay(n, 1)
                    if s.prep and n == 0:
                        if s.core:
                            act.wait_ge(S["log1p"], 2 * p)
                        else:
                            act.wait_ge(S["rstd"], 5)
                        standardise(xn_tok, scale_n, shift_n, "xn_tok")
                    for w in s.finished(n - 2, 2):
                        evacuate(*w)
                    side(2 * n)
                    if s.core and n < N:
                        decay(n, 2)
                        decay(n, 3)
                    for w in s.finished(n - 1, 1):
                        evacuate(*w)
                    side(2 * n + 1)

            run(act, segment)

        @block.gpsimd
        def _(pool):
            def segment(s):
                i, p = s.i, s.p
                for n in range(N + 1):
                    if s.core and n < N:
                        j = i * N + n
                        if n == 0:
                            pool.wait_ge(S["dx"], 2 * (i + 1))
                        if n % 2 == 0:
                            pool.wait_ge(S[f"brow{n // 2 % 2}"], 16 * (i * 4 + n // 4 + 1))
                        if not (s.first and n < 2):
                            pool.wait_ge(S["scan"], (j - 1) * KE)
                        nc.gpsimd.tensor_tensor(
                            u[:, n % 2, :, :], dx[:, s.h, :, :],
                            brow[:, n // 2 % 2, n % 2, :].unsqueeze(1).to_broadcast([P, KE, BANK]),
                            ALU.mult).then_inc(S["u"], 1)
                    if s.prep and due(n, "z_add"):
                        pool.wait_ge(S["z"], p + 1)
                        tiles = x_tok[:, bass.ds(p * HT, HT), :] if not isinstance(p, int) \
                            else x_tok[:, p * HT:(p + 1) * HT, :]
                        nc.gpsimd.tensor_tensor(tiles, tiles, z_tok, ALU.add).then_inc(S["z_added"], 1)
                    for g in due(n, "out_add") if s.out else ():
                        pool.wait_ge(S["work_free"], s.place("out", g) + 1)
                        pool.wait_ge(S["z_added"], i)
                        at = (i - 1) * HT + 2 * g
                        tiles = x_tok[:, bass.ds(at, 2), :] if not isinstance(at, int) else x_tok[:, at:at + 2, :]
                        nc.gpsimd.tensor_tensor(tiles, tiles, th[:, g, :].rearrange("p (a d) -> p a d", d=DIM),
                                                ALU.add).then_inc(S["out_added"], 1)
                    for g in due(n, "log1p") if s.prep else ():
                        cs = slice(2 * g, 2 * g + 2)
                        pool.wait_ge(S["ln"], 2 * p + g + 1)
                        nc.gpsimd.tensor_tensor(dx[:, s.ph, cs], tmp_u[:, cs], dx[:, s.ph, cs],
                                                ALU.subtract).then_inc(S["log1p"], 1)
                    for g in due(n, "dx") if s.prep else ():
                        cs = slice(2 * g, 2 * g + 2)
                        pool.wait_ge(S["delta"], 2 * p + g + 1)
                        nc.gpsimd.tensor_tensor(dx[:, s.ph, cs], delta[:, s.ph, cs], x[:, s.ph, cs],
                                                ALU.mult).then_inc(S["dx"], 1)

            run(pool, segment)

        @block.vector
        def _(dve):
            o = W512["conv"][0]
            nc.vector.tensor_scalar(conv[:, :, :], w512[:, :, o:o + TAPS + 1], 0.5, None, ALU.mult)
            nc.vector.memset(pre[:, :, 0:TAPS - 1], 0.0).then_inc(S["history"], 1)
            nc.vector.memset(one[:, :], 1.0)
            for c in range(KE):
                op = nc.vector.tensor_scalar(diag_d[:, c, :], ident[:, :], col("D", c), None, ALU.mult)
            op.then_inc(S["diag_d"], 1)
            nc.vector.memset(parts[:, :, :], 0.0).then_inc(S["zeroed"], 1)
            dve.wait_ge(S["zeroed"], 1)
            dve.wait_ge(S["root"], 1)
            nc.vector.reciprocal(rstd[:, :], root[:, :]).then_inc(S["rstd"], 1)
            dve.wait_ge(S["rstd"], 1)
            nc.vector.tensor_tensor(square[:, :], rstd[:, :], rstd[:, :], ALU.mult).then_inc(S["square"], 1)
            dve.wait_ge(S["square"], 1)
            nc.vector.tensor_tensor(square[:, :], square[:, :], moments[:, :, 1], ALU.mult).then_inc(S["square"], 1)
            dve.wait_ge(S["root"], 2)
            nc.vector.reciprocal(rrms[:, :], root[:, :]).then_inc(S["rstd"], 1)
            dve.wait_ge(S["rstd"], 2)
            nc.vector.scalar_tensor_tensor(shift[:, :], moments[:, :, 0], -1.0, rstd[:, :], ALU.mult, ALU.mult)\
                .then_inc(S["rstd"], 1)
            nc.vector.tensor_tensor(scale_n[:, :], rstd[:, :], rrms[:, :], ALU.mult).then_inc(S["rstd"], 1)
            dve.wait_ge(S["rstd"], 4)
            nc.vector.tensor_tensor(shift_n[:, :], shift[:, :], rrms[:, :], ALU.mult).then_inc(S["rstd"], 1)

            def segment(s):
                i, p = s.i, s.p

                def scan(n, c):
                    j = i * N + n
                    dve.wait_ge(S["a"], j * KE + c + 1)
                    nc.vector.tensor_tensor_scan(
                        hid[:, n % 2, c, :], bank[4 + c % 2][:, :], u[:, n % 2, c, :],
                        0.0 if s.h == 0 else carry[:, n, c:c + 1], ALU.mult, ALU.add).then_inc(S["scan"], 1)

                def weigh(n, pair):
                    j = i * N + n
                    cs = slice(2 * pair, 2 * pair + 2)
                    if pair == 0:
                        dve.wait_ge(S["scan"], (j + 1) * KE)
                        if s.h == 0:
                            nc.vector.tensor_copy(carry[:, n, :], hid[:, n % 2, :, BANK - 1])\
                                .then_inc(S["carry"], 1)
                        dve.wait_ge(S["c_done"], j + 1)
                        if not (s.first and n < 2):
                            dve.wait_ge(S["y_part"], j - 1)
                    nc.vector.tensor_tensor(hc[:, n % 2, cs, :], hid[:, n % 2, cs, :],
                                            bank[7][:, :].unsqueeze(1).to_broadcast([P, 2, BANK]),
                                            ALU.mult).then_inc(S["hc"], 1)

                def finish():
                    dve.wait_ge(S["y_part"], i * N)
                    dve.wait_ge(S["gate"], i * KE)
                    for c in range(KE):
                        nc.vector.scalar_tensor_tensor(gate[:, c, :], bank[c][:, :], 0.5, gate[:, c, :],
                                                       ALU.mult, ALU.mult).then_inc(S["y"], 1)

                def convolve(c):
                    dve.wait_ge(S["work_free"], s.place("in", c) + 1)
                    a = acc[:, s.ph, c, :]
                    for k in range(TAPS - 1):
                        if k > 0:
                            dve.wait_ge(S["taps"], (p * KE + c) * (TAPS - 2) + k)
                        nc.vector.scalar_tensor_tensor(a, pre[:, c, k:k + BANK], conv[:, c, k:k + 1], a,
                                                       ALU.mult, ALU.add)\
                            .then_inc(S["taps" if k < TAPS - 2 else "conv"], 1)

                def keep_history():
                    dve.wait_ge(S["conv"], (p + 1) * KE)
                    if s.ph == 0:
                        nc.vector.tensor_copy(pre[:, :, 0:TAPS - 1], pre[:, :, BANK:BANK + TAPS - 1])\
                            .then_inc(S["history"], 1)
                    else:
                        nc.vector.memset(pre[:, :, 0:TAPS - 1], 0.0).then_inc(S["history"], 1)
                    dve.wait_ge(S["history"], p + 2)

                def silu(c):
                    dve.wait_ge(S["tanh_x"], p * KE + c + 1)
                    nc.vector.scalar_tensor_tensor(x[:, s.ph, c, :], th_x[:, c, :], 1.0, acc[:, s.ph, c, :],
                                                   ALU.add, ALU.mult).then_inc(S["x"], 1)

                def gate_skip(c):
                    dve.wait_ge(S["work_free"], s.place("skip", c) + 1)
                    nc.vector.scalar_tensor_tensor(gate[:, c, :], th[:, c % 2, :], 1.0, gate[:, c, :],
                                                   ALU.add, ALU.mult).then_inc(S["gate"], 1)

                def split_c(part):
                    R = slice(RANK, RANK + STATE)
                    if part == 0:
                        dve.wait_ge(S["work_free"], s.place("xproj", 0) + 1)
                        nc.vector.tensor_tensor(rest[s.ph][R, :], proj[R, :], parts[R, s.ph, :], ALU.subtract)\
                            .then_inc(S["rest"], 1)
                    else:
                        dve.wait_ge(S["mid"], p + 1)
                        nc.vector.tensor_tensor(parts[32:32 + STATE, s.ph, :], rest[s.ph][R, :], mid[s.ph][R, :],
                                                ALU.subtract).then_inc(S["parts"], 1)

                def round_off(g):
                    cs = slice(2 * g, 2 * g + 2)
                    dve.wait_ge(S["u1"], p * KE + 2 * g + 2)
                    nc.vector.scalar_tensor_tensor(dx[:, s.ph, cs], tmp_u[:, cs], -1.0, dx[:, s.ph, cs],
                                                   ALU.add, ALU.subtract).then_inc(S["corr"], 1)

                def softplus(g):
                    cs = slice(2 * g, 2 * g + 2)
                    dve.wait_ge(S["log1p"], 2 * p + g + 1)
                    nc.vector.scalar_tensor_tensor(delta[:, s.ph, cs], delta[:, s.ph, cs], 0.0, dx[:, s.ph, cs],
                                                   ALU.max, ALU.add).then_inc(S["delta"], 1)

                def side(time):
                    if s.prep:
                        for c in due(time, "conv"):
                            convolve(c)
                            if c == KE - 1:
                                keep_history()
                        for c in due(time, "silu"):
                            silu(c)
                        for part in due(time, "split"):
                            split_c(part)
                        for g in due(time, "corr"):
                            round_off(g)
                        for g in due(time, "softplus"):
                            softplus(g)
                    if s.core:
                        for c in due(time, "gate"):
                            gate_skip(c)

                for n in range(N + 1):
                    if s.core and n < N:
                        j = i * N + n
                        dve.wait_ge(S["u"], j + 1)
                        if n == 0 and s.h == 1:
                            dve.wait_ge(S["carry"], (i + 1) * N // 2 if isinstance(i, int) else (i + 1) * (N // 2))
                        if not (s.first and n < 2):
                            dve.wait_ge(S["hc"], 2 * (j - 1))
                    for pair in range(2):
                        if s.core and n < N:
                            scan(n, 2 * pair)
                            scan(n, 2 * pair + 1)
                        if pair == 0:
                            side(2 * n)
                        if s.core and n > 0:
                            weigh(n - 1, pair)
                    if n == 0 and s.out:
                        finish()
                    side(2 * n + 1)
                    if n == 0 and not s.core and not s.prep:
                        dve.wait_ge(S["out_added"], 2 * 2 * HALVES)
                        for t in range(2 * BT):
                            op = nc.vector.bn_stats(final_stats[:, t, :], x_tok[:, t, :])
                        op.then_inc(S["final_stats"], 1)
                        dve.wait_ge(S["final_stats"], 1)
                        for t in range(2 * BT):
                            nc.vector.bn_aggr(moments[:, t, :], final_stats[:, t, :])

            run(dve, segment)

        @block.tensor
        def _(pe):
            def segment(s):
                i, p = s.i, s.p

                def work(kind, c, part):
                    place = s.place(kind, c)
                    if part > 0:
                        pass
                    elif s.prep and not s.core:
                        former = {"in": ("turn", 1), "dt": ("xproj", 0)}.get(kind)
                        if former:
                            pe.wait_ge(S["work_free"], s.place(*former) + 1)
                    else:
                        pe.wait_ge(S["work_free"], place)
                    b = work_bank(s, kind, c)
                    if kind == "turn":
                        pe.wait_ge(S["xn_tok"], p + 1)
                        for k in range(KD):
                            for t in range(2):
                                op = nc.tensor.transpose(b[:, (2 * k + t) * P:(2 * k + t + 1) * P],
                                                         xn_tok[:, 2 * c + t, k * P:(k + 1) * P], ident[:, :])
                    elif kind in ("in", "skip"):
                        for k in (part,):
                            o = W256[kind][0] + c * P
                            op = nc.tensor.matmul(b[:, :], w256[:, k, o:o + P],
                                                  xn[:, s.ph if kind == "in" else s.h, k, :],
                                                  start=k == 0, stop=k == KD - 1)
                    elif kind == "xproj":
                        for k in (2 * part, 2 * part + 1):
                            pe.wait_ge(S["x"], p * KE + k + 1)
                            op = nc.tensor.matmul(b[0:XROWS, :], col("xproj", k, XROWS), x[:, s.ph, k, :],
                                                  start=k == 0, stop=k == KE - 1)
                    elif kind == "dt":
                        op = nc.tensor.matmul(b[:, :], w64[:, c * P:(c + 1) * P], proj[0:RANK, :],
                                              start=True, stop=True)
                    elif kind == "out":
                        pe.wait_ge(S["y"], i * KE)
                        for t in (part,):
                            for k in range(KE):
                                at = (2 * c + t) * P
                                op = nc.tensor.matmul(b[:, t * DIM:(t + 1) * DIM], gate[:, k, at:at + P],
                                                      col("out", k, DIM), start=k == 0, stop=k == KE - 1)
                    if part == PARTS[kind] - 1:
                        op.then_inc(S["work_done"], 1)

                if s.first:
                    pe.wait_ge(S["diag_d"], 1)
                for n in range(N + 1):
                    j = i * N + n
                    if s.core and n < N:
                        if n == 0:
                            pe.wait_ge(S["parts"], i + 1)
                        if not (s.first and n == 0):
                            pe.wait_ge(S["hc"], 2 * j)
                        nc.tensor.matmul(bank[7][:, :], select[:, n, :], parts[:, s.h, :],
                                         start=True, stop=True).then_inc(S["c_done"], 1)
                    for w in s.at(n, 1):
                        work(*w)
                    if s.core and n > 0:
                        m = n - 1
                        if m == 0 and not s.first:
                            pe.wait_ge(S["y"], i * KE)
                        if m == 0:
                            for c in range(KE):
                                nc.tensor.matmul(bank[c][:, :], diag_d[:, c, :], x[:, s.h, c, :],
                                                 start=True, stop=False)
                        pe.wait_ge(S["hc"], 2 * j)
                        for c in range(KE):
                            op = nc.tensor.matmul(bank[c][:, :], ident[:, :], hc[:, m % 2, c, :],
                                                  start=False, stop=m == N - 1)
                        op.then_inc(S["y_part"], 1)
                    for w in s.at(n, 2):
                        work(*w)

            run(pe, segment)


def build(nc, x_in, w256_in, w512_in, w128_in, w64_in, out):
    with ExitStack() as ctx:
        sb = lambda n, s, d=F32: ctx.enter_context(nc.sbuf_tensor(n, s, d))
        mem = {
            "x_tok": sb("x_tok", [P, TILES, DIM]),
            "w256": sb("w256", [P, KD, W256_COLS]),
            "w512": sb("w512", [P, KE, W512_COLS]),
            "w128": sb("w128", [P, W128_COLS]),
            "w64": sb("w64", [RANK, W64_COLS]),
            "ident": sb("ident", [P, P]),
            "select": sb("select", [RANK + STATE, STATE, P], BF16),
            "sign": sb("sign", [P, 1]),
            "eps": sb("eps", [P, 1]),
            "moments": sb("moments", [P, TILES, 2]),
        }
        load_sem = {n: ctx.enter_context(nc.semaphore(f"load_{n}")) for n in (
            "x", "x0", "x1", "x2", "x3", "weights", "late_weights", "ident", "select")}
        ins = {
            "x": x_in.rearrange("b (t p) d -> p (b t) d", p=P),
            "w256": w256_in.rearrange("(k p) f -> p k f", p=P),
            "w512": w512_in.rearrange("(k p) f -> p k f", p=P),
            "w128": w128_in, "w64": w64_in,
        }
        setup(nc, mem, load_sem, ins)
        ffn(nc, mem, "f1", load_sem, None, measured=(), measure_next=True)
        mamba(nc, mem, nc.dram_tensor("b_rows", [2, STATE, BANK], F32, kind="Internal").ap())
        ffn(nc, mem, "f2", None, out.rearrange("b (t p) d -> p (b t) d", p=P), measured=(0, 1),
            measure_next=False)


def kernel(**inputs):
    import numpy as np
    import concourse.bacc as bacc
    from concourse.bass_utils import run_bass_kernel_spmd

    a = {n: np.asarray(v) for n, v in inputs.items()}
    f = lambda n: a["L0_ffn_" + n]
    m = lambda n: a["L0_attn_" + n]
    col = lambda v: v.reshape(-1, 1)
    rows = lambda v, n: np.broadcast_to(v.reshape(1, -1), (n, v.size))
    arrays = {
        "x_in": m("resid"),
        "w256_in": np.concatenate([m("in_w").T, m("skip_w").T, f("cn_w1"), f("cn_w2"), f("gc_w1")], axis=1),
        "w512_in": np.concatenate([m("wd1").T, m("wC").T, m("wB").T, m("out_w").T, m("conv_w"), col(m("conv_b")),
                                   col(m("W_D")), col(m("wd2_b")), m("A_log")], axis=1),
        "w128_in": np.concatenate([
            f("cn_w3"), f("gc_w2"), np.broadcast_to(np.concatenate([f("cn_w4")] * 2, axis=0), (P, P)),
            col(f("cn_b2")), col(f("gc_b1")), m("norm_w").reshape(KD, P).T, f("cn_b1").reshape(KD, P).T,
            col(np.concatenate([f("cn_b3")] * 2)), rows(f("cn_b4"), P), rows(f("gc_b3"), P),
            rows(f("adaptive_range"), P)], axis=1),
        "w64_in": np.concatenate([m("wd2").T, np.broadcast_to(f("gc_w3"), (H3, P)), col(f("gc_b2"))], axis=1),
    }
    arrays = {n: np.ascontiguousarray(v) for n, v in arrays.items()}
    nc = bacc.Bacc("TRN2", target_bir_lowering=False, num_devices=1)
    args = [nc.dram_tensor(n, v.shape, mybir.dt.from_np(v.dtype), kind="ExternalInput").ap()
            for n, v in arrays.items()]
    out = nc.dram_tensor("out", arrays["x_in"].shape, F32, kind="ExternalOutput").ap()
    build(nc, *args, out)
    return run_bass_kernel_spmd(nc, [arrays], core_ids=[0]).results[0]["out"]
```
